# Optimizing a Trainium2 kernel written in Bass

```python
import numpy as np
import jax
import jax.numpy as jnp

def _softmax(x, axis=-1):
    return jax.nn.softmax(x, axis=axis)
def _gelu(x):
    return jax.nn.gelu(x, approximate=True)
def _silu(x):
    return jax.nn.silu(x)
def _sigmoid(x):
    return jax.nn.sigmoid(x)
def _layernorm(x, axis=-1, eps=1e-5):
    m = jnp.mean(x, axis=axis, keepdims=True)
    v = jnp.var(x, axis=axis, keepdims=True)
    return (x - m) / jnp.sqrt(v + eps)
def _scatter_add(tgt, idx, src, axis=0):
    return tgt.at[idx].add(src)
def _segment_sum(src, seg, n):
    return jax.ops.segment_sum(src, seg, n)

kernel_name = 'mk_adj_resnorm_d4_adj_512_94b99a'

def setup_inputs(seed: int = 0):
    np.random.seed(seed)
    _w = jnp.asarray
    def _rec_inputs():
        import jax
        import jax.numpy as jnp
        _gk = jax.random.key(seed)
        x = -0.0002928 + 1 * jax.random.normal(jax.random.fold_in(_gk, 1), (3327, 512), jnp.float32)
        _a = jax.random.bernoulli(jax.random.fold_in(_gk, 2), 0.00961827, (3327, 3327))
        adj = _a.astype(jnp.int32)
        return x, adj
    x, adj = _rec_inputs()
    def _L0_gnn_setup():
        import jax, jax.numpy as jnp
        import numpy as np
        N, D_IN, D_OUT = (8192, 512, 512)
        key = jax.random.key(seed)
        ks = jax.random.split(key, 8)
        scale_in = 1.0 / np.sqrt(D_IN)
        scale_cat = 1.0 / np.sqrt(2 * D_OUT)
        return {'x': jax.random.normal(ks[0], (N, D_IN), dtype=jnp.float32), 'adj': jax.random.randint(ks[1], (N, N), 0, 2, dtype=jnp.int32), 'W_self': jax.random.uniform(ks[2], (D_IN, D_OUT), jnp.float32, -scale_in, scale_in), 'b_self': jax.random.uniform(ks[3], (D_OUT,), jnp.float32, -scale_in, scale_in), 'W_nb': jax.random.uniform(ks[4], (D_IN, D_OUT), jnp.float32, -scale_in, scale_in), 'b_nb': jax.random.uniform(ks[5], (D_OUT,), jnp.float32, -scale_in, scale_in), 'W_comb': jax.random.uniform(ks[6], (2 * D_OUT, D_OUT), jnp.float32, -scale_cat, scale_cat), 'b_comb': jax.random.uniform(ks[7], (D_OUT,), jnp.float32, -scale_cat, scale_cat)}
    _L0_gnn_all = _L0_gnn_setup()
    _L0_gnn_in = {k: v for k, v in _L0_gnn_all.items() if k in ('W_self', 'b_self', 'W_nb', 'b_nb', 'W_comb', 'b_comb', )}
    del _L0_gnn_all

    def _L1_gnn_setup():
        import jax, jax.numpy as jnp
        import numpy as np
        N = 8192
        IN_F = 512
        OUT_F = 512
        ALPHA = 0.2
        key = jax.random.key(seed)
        k1, k2, k3, k4, k5 = jax.random.split(key, 5)
        inp = jax.random.normal(k1, (N, IN_F), dtype=jnp.float32)
        adj = jax.random.randint(k2, (N, N), 0, 2, dtype=jnp.int32)
        W1 = jax.random.normal(k3, (IN_F, OUT_F), dtype=jnp.float32) * (1.0 / np.sqrt(IN_F))
        b1 = jnp.zeros((OUT_F,), dtype=jnp.float32)
        a = jax.random.normal(k4, (2 * OUT_F,), dtype=jnp.float32) * (1.0 / np.sqrt(2 * OUT_F))
        a1 = a[:OUT_F]
        a2 = a[OUT_F:]
        b2 = jnp.zeros((), dtype=jnp.float32)
        return {'inp': inp, 'adj': adj, 'W1': W1, 'b1': b1, 'a1': a1, 'a2': a2, 'b2': b2}
    _L1_gnn_all = _L1_gnn_setup()
    _L1_gnn_in = {k: v for k, v in _L1_gnn_all.items() if k in ('W1', 'b1', 'a1', 'a2', 'b2', )}
    del _L1_gnn_all

    def _L2_gnn_setup():
        import jax, jax.numpy as jnp
        import numpy as np
        N, IN_DIM, HEADS, OUT_DIM = (3072, 512, 8, 64)
        ALPHA = 0.2
        NEG_INF = jnp.float32(-9000000000000000.0)
        key = jax.random.key(seed)
        k1, k2, k3, k4, k5 = jax.random.split(key, 5)
        x = jax.random.normal(k1, (N, IN_DIM), dtype=jnp.float32)
        adj = jax.random.randint(k2, (N, N), 0, 2, dtype=jnp.int32)
        bw = 1.414 * float(np.sqrt(6.0 / (IN_DIM + OUT_DIM)))
        W = jax.random.uniform(k3, (HEADS, IN_DIM, OUT_DIM), dtype=jnp.float32, minval=-bw, maxval=bw)
        ba = 1.414 * float(np.sqrt(6.0 / (2 * OUT_DIM + 1)))
        a1 = jax.random.uniform(k4, (HEADS, OUT_DIM), dtype=jnp.float32, minval=-ba, maxval=ba)
        a2 = jax.random.uniform(k5, (HEADS, OUT_DIM), dtype=jnp.float32, minval=-ba, maxval=ba)
        return {'x': x, 'adj': adj, 'W': W, 'a1': a1, 'a2': a2}
    _L2_gnn_all = _L2_gnn_setup()
    _L2_gnn_in = {k: v for k, v in _L2_gnn_all.items() if k in ('W', 'a1', 'a2', )}
    del _L2_gnn_all

    def _L3_gnn_setup():
        import jax, jax.numpy as jnp
        import numpy as np
        IN_F, OUT_F, HEADS = (512, 64, 8)
        ALPHA = 0.2
        NEG_INF = -9000000000000000.0

        def _xavier(key, shape, gain=1.414):
            fan_in, fan_out = (shape[-2], shape[-1])
            limit = gain * np.sqrt(6.0 / (fan_in + fan_out))
            return jax.random.uniform(key, shape, jnp.float32, -limit, limit)
        key = jax.random.key(seed)
        k_h, k_adj, k_W, k_a = jax.random.split(key, 4)
        N = 4096
        h = jax.random.normal(k_h, (N, IN_F), jnp.float32)
        adj = jax.random.randint(k_adj, (N, N), 0, 2, jnp.int32)
        W = _xavier(k_W, (HEADS, IN_F, OUT_F))
        a = _xavier(k_a, (HEADS, 2 * OUT_F, 1))[..., 0]
        return {'h': h, 'adj': adj, 'W': W, 'a': a}
    _L3_gnn_all = _L3_gnn_setup()
    _L3_gnn_in = {k: v for k, v in _L3_gnn_all.items() if k in ('W', 'a', )}
    del _L3_gnn_all

    return {
        "x": x,
        "adj": adj,
        "L0_gnn_W_self": _L0_gnn_in["W_self"],
        "L0_gnn_b_self": _L0_gnn_in["b_self"],
        "L0_gnn_W_nb": _L0_gnn_in["W_nb"],
        "L0_gnn_b_nb": _L0_gnn_in["b_nb"],
        "L0_gnn_W_comb": _L0_gnn_in["W_comb"],
        "L0_gnn_b_comb": _L0_gnn_in["b_comb"],
        "L1_gnn_W1": _L1_gnn_in["W1"],
        "L1_gnn_b1": _L1_gnn_in["b1"],
        "L1_gnn_a1": _L1_gnn_in["a1"],
        "L1_gnn_a2": _L1_gnn_in["a2"],
        "L1_gnn_b2": _L1_gnn_in["b2"],
        "L2_gnn_W": _L2_gnn_in["W"],
        "L2_gnn_a1": _L2_gnn_in["a1"],
        "L2_gnn_a2": _L2_gnn_in["a2"],
        "L3_gnn_W": _L3_gnn_in["W"],
        "L3_gnn_a": _L3_gnn_in["a"],
    }

def reference(x, adj, L0_gnn_W_self, L0_gnn_b_self, L0_gnn_W_nb, L0_gnn_b_nb, L0_gnn_W_comb, L0_gnn_b_comb, L1_gnn_W1, L1_gnn_b1, L1_gnn_a1, L1_gnn_a2, L1_gnn_b2, L2_gnn_W, L2_gnn_a1, L2_gnn_a2, L3_gnn_W, L3_gnn_a):
    import jax
    import jax.numpy as jnp
    def _L0_gnn_ref(x, adj, W_self, b_self, W_nb, b_nb, W_comb, b_comb):
        import jax, jax.numpy as jnp
        import numpy as np
        N, D_IN, D_OUT = (8192, 512, 512)
        mask = (adj > 0).astype(x.dtype)
        deg = jnp.sum(mask, axis=1, keepdims=True)
        agg = mask @ x / jnp.maximum(deg, 1.0)
        self_f = x @ W_self + b_self
        nb_f = agg @ W_nb + b_nb
        combined = jnp.concatenate([self_f, nb_f], axis=-1)
        out = combined @ W_comb + b_comb
        return jax.nn.relu(out)

    def _L1_gnn_ref(inp, adj, W1, b1, a1, a2, b2):
        import jax, jax.numpy as jnp
        import numpy as np
        N = 8192
        IN_F = 512
        OUT_F = 512
        ALPHA = 0.2
        h = inp @ W1 + b1
        e = jax.nn.leaky_relu((h @ a1)[:, None] + (h @ a2)[None, :] + b2, ALPHA)
        attention = jnp.where(adj > 0, e, jnp.float32(-1000000000000.0))
        attention = jax.nn.softmax(attention, axis=1)
        h_prime = attention @ h
        return jax.nn.elu(h_prime)

    def _L2_gnn_ref(x, adj, W, a1, a2):
        import jax, jax.numpy as jnp
        import numpy as np
        N, IN_DIM, HEADS, OUT_DIM = (3072, 512, 8, 64)
        ALPHA = 0.2
        NEG_INF = jnp.float32(-9000000000000000.0)
        Wh = jnp.einsum('nd,hdo->hno', x, W)
        f1 = jnp.einsum('hno,ho->hn', Wh, a1)
        f2 = jnp.einsum('hno,ho->hn', Wh, a2)
        e = jax.nn.leaky_relu(f1[:, :, None] + f2[:, None, :], negative_slope=ALPHA)
        e = jnp.where(adj[None, :, :] > 0, e, NEG_INF)
        attention = jax.nn.softmax(e, axis=-1)
        h_prime = jnp.einsum('hnm,hmo->hno', attention, Wh)
        out = jax.nn.elu(h_prime)
        return jnp.transpose(out, (1, 0, 2)).reshape(x.shape[0], HEADS * OUT_DIM)

    def _L3_gnn_ref(h, adj, W, a):
        import jax, jax.numpy as jnp
        import numpy as np
        IN_F, OUT_F, HEADS = (512, 64, 8)
        ALPHA = 0.2
        NEG_INF = -9000000000000000.0

        def _xavier(key, shape, gain=1.414):
            fan_in, fan_out = (shape[-2], shape[-1])
            limit = gain * np.sqrt(6.0 / (fan_in + fan_out))
            return jax.random.uniform(key, shape, jnp.float32, -limit, limit)
        Wh = jnp.einsum('ni,hio->hno', h, W)
        a1, a2 = (a[:, :OUT_F], a[:, OUT_F:])
        f1 = jnp.einsum('hno,ho->hn', Wh, a1)
        f2 = jnp.einsum('hno,ho->hn', Wh, a2)
        e = jax.nn.leaky_relu(f1[:, :, None] + f2[:, None, :], ALPHA)
        masked = jnp.where(adj[None] > 0, e, NEG_INF)
        attention = jax.nn.softmax(masked, axis=-1)
        h_prime = jnp.einsum('hnm,hmo->hno', attention, Wh)
        return jnp.transpose(h_prime, (1, 0, 2)).reshape(h.shape[0], HEADS * OUT_F)

    x = _layernorm(x + _L0_gnn_ref(x, adj, L0_gnn_W_self, L0_gnn_b_self, L0_gnn_W_nb, L0_gnn_b_nb, L0_gnn_W_comb, L0_gnn_b_comb), axis=-1)
    x = _layernorm(x + _L1_gnn_ref(x, adj, L1_gnn_W1, L1_gnn_b1, L1_gnn_a1, L1_gnn_a2, L1_gnn_b2), axis=-1)
    x = _layernorm(x + _L2_gnn_ref(x, adj, L2_gnn_W, L2_gnn_a1, L2_gnn_a2), axis=-1)
    x = _layernorm(x + _L3_gnn_ref(x, adj, L3_gnn_W, L3_gnn_a), axis=-1)
    return x


_drawn_inputs = setup_inputs


def setup_inputs(seed=0):
    import zlib

    import numpy as np

    out = dict(_drawn_inputs(seed))
    spreads = {'L1_gnn_b1': (0.0, 0.1)}
    factors = {'L0_gnn_b_self': 3.588, 'L0_gnn_b_nb': 2.99}
    for name, (base, spread) in spreads.items():
        noise = np.random.default_rng([zlib.crc32(name.encode()), seed]).standard_normal(out[name].shape)
        drawn = base * np.exp(spread * noise) if base else spread * noise
        out[name] = jnp.asarray(drawn.astype(out[name].dtype))
    for name, factor in factors.items():
        out[name] = (out[name] * factor).astype(out[name].dtype)
    return out
```

```python
from contextlib import ExitStack

import concourse.bass as bass
from concourse import mybir

ALU = mybir.AluOpType
ACT = mybir.ActivationFunctionType
AX = mybir.AxisListType.X
F32 = mybir.dt.float32
BF16 = mybir.dt.bfloat16
I32 = mybir.dt.int32
U8 = mybir.dt.uint8
RMAX = bass.bass_isa.ReduceOp.max

P = 128
BANK = 512
N = 3327
T = -(-N // P)
NP = T * P
LAST = N - (T - 1) * P
D = 512
C = D // P
SLOPE = 0.2
EPS = 1e-5
B_SHIFT = 30.0
U_SHIFT = 60.0
R_TOP = 45.0


class Chain:

    def __init__(self, eng, sem):
        self.eng, self.sem, self.base, self.n = eng, sem, 0, 0

    def at(self, base):
        self.base, self.n = base, 0

    def link(self, ins):
        ins.then_inc(self.sem, 1)
        self.n += 1
        self.eng.wait_ge(self.sem, self.base + self.n)


def each_tile(eng, step):
    with eng.Fori(0, T // 2 - 1) as pair:
        for p in range(2):
            step(pair * 2 + p, p, False)
    for p in range(2):
        step(T - 2 + p, p, p == 1)


def row_tile(dram, t):
    return dram.rearrange("(t p) d -> t p d", p=P)[t]


def gnn_kernel(nc, x, adj, L0_gnn_W_self, L0_gnn_b_self, L0_gnn_W_nb, L0_gnn_b_nb, L0_gnn_W_comb, L0_gnn_b_comb,
               L1_gnn_W1, L1_gnn_b1, L1_gnn_a1, L1_gnn_a2, L1_gnn_b2, L2_gnn_W, L2_gnn_a1, L2_gnn_a2,
               L3_gnn_W, L3_gnn_a, out):
    with ExitStack() as ctx:
        m = Memory(nc, ctx)
        with ExitStack() as first:
            m.zs = first.enter_context(nc.sbuf_tensor("zs", [P, T, 3, D], BF16))
            with ExitStack() as s:
                fold_weights(nc, s, m, L0_gnn_W_self, L0_gnn_b_self, L0_gnn_W_nb, L0_gnn_b_nb,
                             L0_gnn_W_comb, L0_gnn_b_comb)
                m.end_stage()
                project_input(nc, s, m, x)
            m.end_stage()
            with ExitStack() as s:
                aggregate(nc, s, m, x, adj)
            m.end_stage()
        m.attention_state(nc, ctx)
        head = lambda w: w.rearrange("h d o -> d h o")
        layers = [
            dict(H=1, W=L1_gnn_W1, a1=L1_gnn_a1.rearrange("(h o) -> h o", h=1),
                 a2=L1_gnn_a2.rearrange("(h o) -> h o", h=1), b1=L1_gnn_b1, b2=L1_gnn_b2, elu=True),
            dict(H=8, W=head(L2_gnn_W), a1=L2_gnn_a1, a2=L2_gnn_a2, b1=None, b2=None, elu=True),
            dict(H=8, W=head(L3_gnn_W), a1=L3_gnn_a[:, 0:64], a2=L3_gnn_a[:, 64:128], b1=None, b2=None, elu=False),
        ]
        for n, layer in enumerate(layers, 1):
            with ExitStack() as s:
                project(nc, s, m, f"L{n}", layer)
            m.end_stage()
            with ExitStack() as s:
                if layer["H"] == 1:
                    attend_one_head(nc, s, m, f"L{n}")
                else:
                    attend_heads(nc, s, m, f"L{n}", layer["H"])
            m.end_stage()
            if layer["H"] > 1:
                with ExitStack() as s:
                    finish_heads(nc, s, m, f"L{n}", layer["H"], layer["elu"])
                m.end_stage()
        with ExitStack() as s:
            normalise_out(nc, s, m, out)


class Memory:

    def __init__(self, nc, ctx):
        sb = lambda n, s, d: ctx.enter_context(nc.sbuf_tensor(n, s, d))
        dram = lambda n, s: nc.dram_tensor(n, s, F32, kind="Internal").ap()
        self.mask = sb("mask", [P, T, NP], U8)
        self.ident = sb("ident", [P, P], F32)
        self.identb = sb("identb", [P, P], BF16)
        self.empty = sb("empty", [P, T], F32)
        self.stats = sb("stats", [P, T, 6], F32)
        self.y = dram("y_scratch", [NP, D])
        self.x = dram("x_scratch", [NP, D])
        self.self_part = dram("self_scratch", [NP, D])
        self.h = dram("h_scratch", [NP, D])
        self.rows = dram("r_scratch", [8, NP])
        self.num = dram("num_scratch", [8, 64, NP])
        self.den = dram("den_scratch", [8, NP])
        self.nc, self.stage_sems = nc, []

    def sem(self, name):
        self.stage_sems.append(self.nc.alloc_semaphore(name=name))
        return self.stage_sems[-1]

    def end_stage(self):
        self.nc.clear_and_free_semaphores(self.stage_sems)
        self.stage_sems = []
        self.nc.all_engine_barrier()

    def attention_state(self, nc, ctx):
        sb = lambda n, s, d: ctx.enter_context(nc.sbuf_tensor(n, s, d))
        self.u = sb("u", [P, 8, T], F32)
        self.b = sb("b", [P, 8, T], F32)
        self.mean_h = sb("mean_h", [P, D], F32)


def fold_weights(nc, ctx, m, w_self, b_self, w_nb, b_nb, w_comb, b_comb):
    sb = lambda n, s, d=F32: ctx.enter_context(nc.sbuf_tensor(n, s, d))
    m.fold = sb("fold", [P, 2, C, D])
    m.fold_bias = sb("fold_bias", [P, D])
    with ExitStack() as s2:
        sb = lambda n, s, d=F32: s2.enter_context(nc.sbuf_tensor(n, s, d))
        ps = lambda n, s: s2.enter_context(nc.psum_tensor(n, s, F32))
        space = m.zs[:].rearrange("p t s d -> p (t s d)").bitcast(F32)
        size = 2 * C * D
        w_in, wT, wc = (space[:, n * size:(n + 1) * size].rearrange("p (w c n) -> p w c n", w=2, c=C) for n in range(3))
        bias_col = sb("bias_col", [P, 2, C])
        bias_wide = sb("bias_wide", [P, 2, C, P])
        bias_comb = sb("bias_comb", [P, D])
        ones = sb("ones_row", [P, P])
        pT = ps("pT", [P, 2, BANK])
        pF = ps("pF", [P, 2, BANK])
        pB = ps("pB", [P, BANK])
        loaded, zeroed, ident_ready, wide, transposed, copied, product, product_used, bias_done, done = (
            m.sem("fw_" + n) for n in ("loaded", "zeroed", "ident", "wide", "transposed", "copied", "product",
                                       "product_used", "bias_done", "done"))
        with nc.Block() as block:
            @block.sync
            def _(sp):
                sp.dma_start(w_in[:, 0], w_self.rearrange("(c p) n -> p c n", p=P)).then_inc(loaded, 16)
                sp.dma_start(w_in[:, 1], w_nb.rearrange("(c p) n -> p c n", p=P)).then_inc(loaded, 16)
                sp.dma_start(wc[:, 0], w_comb[0:D].rearrange("(c p) n -> p c n", p=P)).then_inc(loaded, 16)
                sp.dma_start(wc[:, 1], w_comb[D:2 * D].rearrange("(c p) n -> p c n", p=P)).then_inc(loaded, 16)
                with nc.allow_non_contiguous_dma("two small bias columns"):
                    sp.dma_start(bias_col[:, 0], b_self.rearrange("(c p) -> p c", p=P)).then_inc(loaded, 16)
                    sp.dma_start(bias_col[:, 1], b_nb.rearrange("(c p) -> p c", p=P)).then_inc(loaded, 16)
                sp.dma_start(bias_comb[:], b_comb.partition_broadcast(P)).then_inc(loaded, 16)
                sp.wait_ge(loaded, 7 * 16)

            @block.gpsimd
            def _(pool):
                nc.gpsimd.memset(m.ident[:], 0.0).then_inc(zeroed, 1)
                nc.gpsimd.memset(m.identb[:], 0.0).then_inc(zeroed, 1)
                pool.wait_ge(zeroed, 2)
                for t in (m.ident, m.identb):
                    nc.gpsimd.affine_select(out=t[:], in_=t[:], compare_op=ALU.not_equal, fill=1.0, base=0,
                                            pattern=[[-1, P]], channel_multiplier=1).then_inc(ident_ready, 1)

            @block.vector
            def _(dve):
                nc.vector.memset(ones[:], 1.0).then_inc(wide, 1)
                dve.wait_ge(wide, 1)
                dve.wait_ge(loaded, 7 * 16)
                for w in range(2):
                    for c in range(C):
                        nc.vector.tensor_scalar(bias_wide[:, w, c], ones[:], bias_col[:, w, c:c + 1], None,
                                                ALU.mult).then_inc(wide, 1)
                for n in range(2 * C):
                    dve.wait_ge(product, n + 1)
                    nc.vector.tensor_copy(m.fold[:, n // C, n % C], pF[:, n % 2]).then_inc(product_used, 1)
                dve.wait_ge(bias_done, 1)
                nc.vector.tensor_tensor(m.fold_bias[:], pB[:], bias_comb[:], ALU.add).then_inc(done, 1)

            @block.scalar
            def _(act):
                for n in range(2 * C):
                    act.wait_ge(transposed, n + 1)
                    nc.scalar.activation(wT[:, n // C, n % C], pT[:, n % 2], ACT.Copy).then_inc(copied, 1)

            @block.tensor
            def _(pe):
                pe.wait_ge(ident_ready, 2)
                pe.wait_ge(loaded, 7 * 16)
                for n in range(2 * C):
                    w, c = n // C, n % C
                    if n >= 2:
                        pe.wait_ge(copied, n - 1)
                    for k in range(C):
                        last = nc.tensor.transpose(pT[:, n % 2, k * P:(k + 1) * P],
                                                   w_in[:, w, k, c * P:(c + 1) * P], m.ident[:])
                    last.then_inc(transposed, 1)
                pe.wait_ge(copied, 2 * C)
                for n in range(2 * C):
                    w, k = n // C, n % C
                    if n >= 2:
                        pe.wait_ge(product_used, n - 1)
                    for c in range(C):
                        last = nc.tensor.matmul(pF[:, n % 2], wT[:, w, c, k * P:(k + 1) * P], wc[:, w, c],
                                                start=c == 0, stop=c == C - 1)
                    last.then_inc(product, 1)
                pe.wait_ge(wide, 2 * C + 1)
                for n in range(2 * C):
                    last = nc.tensor.matmul(pB[:], bias_wide[:, n // C, n % C], wc[:, n // C, n % C],
                                            start=n == 0, stop=n == 2 * C - 1)
                last.then_inc(bias_done, 1)


def project_input(nc, ctx, m, x):
    sb = lambda n, s, d=F32: ctx.enter_context(nc.sbuf_tensor(n, s, d))
    ps = lambda n, s: ctx.enter_context(nc.psum_tensor(n, s, F32))
    x_in = sb("pi_x", [P, 2, D])
    xT = sb("pi_xT", [P, 2, C, P])
    self_out = sb("pi_self", [P, 2, D])
    rest = sb("pi_rest", [P, 2, D])
    pT, pS, pZ = ps("pi_pT", [P, 2, BANK]), ps("pi_pS", [P, 2, BANK]), ps("pi_pZ", [P, 2, BANK])
    x_here = [m.sem(f"pi_x_here{p}") for p in range(2)]
    stored = [m.sem(f"pi_stored{p}") for p in range(2)]
    cleared, transposed, xT_ready, self_ready, self_made, z_ready, z_top, pZ_read, chain = (
        m.sem("pi_" + n) for n in ("cleared", "transposed", "xT_ready", "self_ready", "self_made", "z_ready", "z_top",
                                   "pZ_read", "chain"))
    with nc.Block() as block:
        @block.sync
        def _(sp):
            sp.wait_ge(cleared, 1)

            def load(t, p, is_last):
                sp.wait_ge(transposed, t + 1)
                if is_last:
                    sp.dma_start(x_in[0:LAST, p], x[(T - 1) * P:N]).then_inc(x_here[p], 16)
                else:
                    full = x[0:(T - 1) * P].rearrange("(t p) d -> t p d", p=P)
                    sp.dma_start(x_in[:, p], full[t]).then_inc(x_here[p], 16)

            each_tile(sp, load)

        @block.gpsimd
        def _(pool):
            nc.gpsimd.memset(x_in[:], 0.0).then_inc(cleared, 1)

        @block.tensor
        def _(pe):
            def transposes(t, p):
                pe.wait_ge(x_here[p], (t - p) * 8 + 16)
                pe.wait_ge(xT_ready, t + 1)
                for c in range(C):
                    last = nc.tensor.transpose(pT[:, p, c * P:(c + 1) * P], x_in[:, p, c * P:(c + 1) * P], m.ident[:])
                last.then_inc(transposed, 1)

            def products(t, p, is_last):
                if not is_last:
                    transposes(t + 1, 1 - p)
                pe.wait_ge(xT_ready, t + 3)
                pe.wait_ge(self_made, t + 1)
                for c in range(C):
                    last = nc.tensor.matmul(pS[:, p], xT[:, p, c], m.fold[:, 0, c], start=c == 0, stop=c == C - 1)
                last.then_inc(self_ready, 1)
                pe.wait_ge(pZ_read, t + 1)
                for c in range(C):
                    last = nc.tensor.matmul(pZ[:, p], xT[:, p, c], m.fold[:, 1, c], start=c == 0, stop=c == C - 1)
                last.then_inc(z_ready, 1)

            pe.sem_inc(transposed, 2)
            pe.sem_inc(z_ready, 2)
            transposes(0, 0)
            each_tile(pe, products)

        @block.scalar
        def _(act):
            act.sem_inc(xT_ready, 2)

            def copy_xT(t, p):
                act.wait_ge(transposed, t + 3)
                act.wait_ge(z_ready, t + 1)
                nc.scalar.activation(xT[:, p].rearrange("p c i -> p (c i)"), pT[:, p], ACT.Copy).then_inc(xT_ready, 1)

            def step(t, p, is_last):
                if not is_last:
                    copy_xT(t + 1, 1 - p)
                act.wait_ge(z_ready, t + 3)
                nc.scalar.activation(m.zs[:, t, 0], pZ[:, p], ACT.Copy).then_inc(z_top, 1)
                act.wait_ge(self_made, t + 3)
                act.dma_start(row_tile(m.self_part, t), self_out[:, p]).then_inc(stored[p], 16)

            copy_xT(0, 0)
            each_tile(act, step)
            for p in range(2):
                act.wait_ge(stored[p], 16 * (T // 2 + 1))

        @block.vector
        def _(dve):
            dve.sem_inc(self_made, 2)
            dve.sem_inc(pZ_read, 2)
            for p in range(2):
                dve.sem_inc(stored[p], 16)
            own = Chain(dve, chain)

            def step(t, p, is_last):
                own.at(t)
                dve.wait_ge(self_ready, t + 1)
                dve.wait_ge(stored[p], (t - p) * 8 + 16)
                nc.vector.tensor_tensor(self_out[:, p], pS[:, p], m.fold_bias[:], ALU.add).then_inc(self_made, 1)
                dve.wait_ge(z_top, t + 1)
                nc.vector.tensor_tensor(rest[:, p], pZ[:, p], m.zs[:, t, 0], ALU.subtract).then_inc(pZ_read, 1)
                dve.wait_ge(pZ_read, t + 3)
                own.link(nc.vector.tensor_copy(m.zs[:, t, 1], rest[:, p]))
                nc.vector.tensor_tensor(m.zs[:, t, 2], rest[:, p], m.zs[:, t, 1], ALU.subtract)

            each_tile(dve, step)


def aggregate(nc, ctx, m, x, adj):
    sb = lambda n, s, d=F32: ctx.enter_context(nc.sbuf_tensor(n, s, d))
    HALF = NP // 2
    GROUP = 8
    GROUPS = -(-T // GROUP)
    adj_in = sb("ag_adj", [P, 2, HALF], I32)
    masked = sb("ag_masked", [P, NP], BF16)
    maskT = sb("ag_maskT", [P, 2, T, P], BF16)
    x_in = sb("ag_x", [P, D])
    self_in = sb("ag_self", [P, D])
    y = sb("ag_y", [P, D])
    degree = sb("ag_degree", [P, T, 2])
    small = sb("ag_small", [P, 2])
    part = sb("ag_part", [P, D])
    pT = ctx.enter_context(nc.psum_tensor("ag_pT", [P, 2, GROUP, P], BF16))
    pA = ctx.enter_context(nc.psum_tensor("ag_pA", [P, 2, BANK], F32))
    adj_here = [m.sem(f"ag_adj_here{h}") for h in range(2)]
    cleared, adj_masked, transposed, maskT_ready, stored_mask, aggregated, pA_read, rows_here, rows_used, y_ready, \
        y_stored, chain = (m.sem("ag_" + n) for n in (
            "cleared", "adj_masked", "transposed", "maskT_ready", "stored_mask", "aggregated", "pA_read", "rows_here",
            "rows_used", "y_ready", "y_stored", "chain"))
    with nc.Block() as block:
        @block.sync
        def _(sp):
            sp.wait_ge(cleared, 2)

            def load(t, p, is_last):
                for h in range(2):
                    cols = HALF if h == 0 else N - HALF
                    sp.wait_ge(adj_masked, t * 2 + h + 1)
                    if is_last:
                        sp.dma_start(adj_in[0:LAST, h, 0:cols], adj[(T - 1) * P:N, h * HALF:h * HALF + cols])\
                          .then_inc(adj_here[h], 16)
                    else:
                        full = adj[0:(T - 1) * P].rearrange("(t p) j -> t p j", p=P)
                        sp.dma_start(adj_in[:, h, 0:cols], full[t][:, h * HALF:h * HALF + cols])\
                          .then_inc(adj_here[h], 16)

            each_tile(sp, load)

        @block.gpsimd
        def _(pool):
            pool.memset(x_in[:], 0.0).then_inc(cleared, 1)

            def step(t, p, is_last):
                pool.wait_ge(maskT_ready, (t + 1) * GROUPS + 2)
                nc.gpsimd.tensor_copy(m.mask[:, :, bass.ts(t, P)], maskT[:, p]).then_inc(stored_mask, 1)

            pool.sem_inc(stored_mask, 2)
            each_tile(pool, step)

        @block.scalar
        def _(act):
            act.wait_ge(cleared, 2)

            def rows(t, is_last):
                act.wait_ge(rows_used, t + 1)
                if is_last:
                    act.dma_start(x_in[0:LAST], x[(T - 1) * P:N]).then_inc(rows_here, 16)
                else:
                    full = x[0:(T - 1) * P].rearrange("(t p) d -> t p d", p=P)
                    act.dma_start(x_in[:], full[t]).then_inc(rows_here, 16)
                act.dma_start(self_in[:], row_tile(m.self_part, t)).then_inc(rows_here, 16)

            def copies(t, p):
                act.wait_ge(aggregated, t + 1)
                act.wait_ge(stored_mask, t + 1)
                for g in range(GROUPS):
                    k = min(GROUP, T - g * GROUP)
                    act.wait_ge(transposed, t * GROUPS + g + 1)
                    nc.scalar.activation(maskT[:, p, g * GROUP:g * GROUP + k], pT[:, g % 2, 0:k],
                                         ACT.Copy).then_inc(maskT_ready, 1)

            def step(t, p, is_last):
                rows(t, is_last)
                if not is_last:
                    copies(t + 1, 1 - p)
                act.wait_ge(y_ready, t + 1)
                act.dma_start(row_tile(m.y, t), y[:]).then_inc(y_stored, 16)

            act.sem_inc(maskT_ready, 2)
            copies(0, 0)
            each_tile(act, step)
            act.wait_ge(y_stored, 16 * (T + 1))

        @block.tensor
        def _(pe):
            def transposes(t, p):
                for g in range(GROUPS):
                    k = min(GROUP, T - g * GROUP)
                    if g == 0:
                        pe.wait_ge(adj_masked, t * 2 + 4)
                    pe.wait_ge(maskT_ready, t * GROUPS + g + 1)
                    for c in range(k):
                        last = nc.tensor.transpose(pT[:, g % 2, c], masked[:, bass.ts(g * GROUP + c, P)], m.identb[:])
                    last.then_inc(transposed, 1)

            def step(t, p, is_last):
                if not is_last:
                    transposes(t + 1, 1 - p)
                pe.wait_ge(maskT_ready, (t + 1) * GROUPS + 2)
                pe.wait_ge(pA_read, t + 1)
                for j in range(T):
                    for part in range(3):
                        last = nc.tensor.matmul(pA[:, p], maskT[:, p, j], m.zs[:, j, part],
                                                start=j == 0 and part == 0, stop=j == T - 1 and part == 2)
                last.then_inc(aggregated, 1)

            pe.sem_inc(aggregated, 2)
            transposes(0, 0)
            each_tile(pe, step)

        @block.vector
        def _(dve):
            own = Chain(dve, chain)
            nc.vector.memset(adj_in[:], 0).then_inc(cleared, 1)
            dve.sem_inc(adj_masked, 2)
            dve.sem_inc(pA_read, 2)
            dve.sem_inc(rows_used, 1)
            dve.sem_inc(y_stored, 16)

            def mask_rows(t):
                if not isinstance(t, int) or t > 0:
                    dve.wait_ge(transposed, t * GROUPS)
                for h in range(2):
                    dve.wait_ge(adj_here[h], (t + 1) * 16)
                    nc.vector.tensor_scalar(masked[:, h * HALF:(h + 1) * HALF], adj_in[:, h], 0.0, 0.0, ALU.is_gt,
                                            ALU.add, accum_out=degree[:, t, h:h + 1]).then_inc(adj_masked, 1)

            def step(t, p, is_last):
                if not is_last and not (isinstance(t, int) and t + 2 >= T):
                    mask_rows(t + 2)
                own.at(t * 5)
                dve.wait_ge(adj_masked, t * 2 + 4)
                own.link(nc.vector.tensor_tensor(small[:, 0:1], degree[:, t, 0:1], degree[:, t, 1:2], ALU.add))
                own.link(nc.vector.tensor_scalar(m.empty[:, bass.ts(t, 1)], small[:, 0:1], 0.0, None, ALU.is_equal))
                own.link(nc.vector.tensor_scalar(small[:, 0:1], small[:, 0:1], 1.0, None, ALU.max))
                own.link(nc.vector.reciprocal(small[:, 1:2], small[:, 0:1]))
                dve.wait_ge(aggregated, t + 3)
                dve.wait_ge(rows_here, (t + 1) * 32)
                nc.vector.scalar_tensor_tensor(out=part[:], in0=pA[:, p], scalar=small[:, 1:2], in1=self_in[:],
                                               op0=ALU.mult, op1=ALU.add).then_inc(pA_read, 1)
                dve.wait_ge(pA_read, t + 3)
                dve.wait_ge(y_stored, (t + 1) * 16)
                nc.vector.scalar_tensor_tensor(out=y[:], in0=part[:], scalar=0.0, in1=x_in[:],
                                               op0=ALU.max, op1=ALU.add).then_inc(y_ready, 1)
                dve.wait_ge(y_ready, t + 1)
                dve.sem_inc(rows_used, 1)
                own.link(nc.vector.bn_stats(m.stats[:, t], y[:]))

            mask_rows(0)
            mask_rows(1)
            each_tile(dve, step)


def load_moments(nc, dve, own, m, mean, rstd, work, std_ready):
    st = m.stats
    v = nc.vector
    own.link(v.tensor_tensor(mean[:], st[:, :, 1], st[:, :, 4], ALU.add))
    own.link(v.tensor_tensor(work[:], st[:, :, 1], st[:, :, 4], ALU.subtract))
    own.link(v.tensor_scalar(mean[:], mean[:], 0.5, None, ALU.mult))
    own.link(v.tensor_scalar(work[:], work[:], 0.5, None, ALU.mult))
    own.link(v.tensor_tensor(work[:], work[:], work[:], ALU.mult))
    own.link(v.tensor_tensor(rstd[:], st[:, :, 2], st[:, :, 5], ALU.add))
    own.link(v.tensor_scalar(rstd[:], rstd[:], 1.0 / D, EPS, ALU.mult, ALU.add))
    own.link(v.tensor_tensor(work[:], work[:], rstd[:], ALU.add))
    std_ready(work)


MOMENT_LINKS = 8


def project(nc, ctx, m, name, layer):
    H, b1, b2 = layer["H"], layer["b1"], layer["b2"]
    O = D // H
    PARTS = 2 if H > 1 else 1
    ROWS = H * T // PARTS
    sb = lambda n, s, d=F32: ctx.enter_context(nc.sbuf_tensor(f"{name}p_{n}", s, d))
    ps = lambda n, s: ctx.enter_context(nc.psum_tensor(f"{name}p_{n}", s, F32))
    W = sb("W", [P, C, D])
    a1, a2 = sb("a1", [P, H, O]), sb("a2", [P, H, O])
    b1_wide = sb("b1", [P, D])
    b2_wide = sb("b2", [P, 1])
    y_in, x_out = sb("y", [P, 2, D]), sb("x", [P, 2, D])
    xT = sb("xT", [P, 2, C, P])
    h_out = sb("h", [P, 2, D])
    prod = sb("prod", [P, 2, D])
    h_sum = sb("h_sum", [P, D])
    f1, f2, R = sb("f1", [P, H, T]), sb("f2", [P, H, T]), sb("R", [P, H, T])
    f2_top, f2_max = sb("f2_top", [P, H]), sb("f2_max", [P, H])
    mean, rstd, work = sb("mean", [P, T]), sb("rstd", [P, T]), sb("work", [P, T])
    over_n = sb("over_n", [P, P])
    rT = sb("rT", [P, 2, P])
    pT, pH = ps("pT", [P, 2, BANK]), ps("pH", [P, 2, BANK])
    pR, pM = ps("pR", [P, 2, BANK]), ps("pM", [P, BANK])
    y_here = [m.sem(f"{name}p_y_here{p}") for p in range(2)]
    x_stored = [m.sem(f"{name}p_x_stored{p}") for p in range(2)]
    h_stored = [m.sem(f"{name}p_h_stored{p}") for p in range(2)]
    loaded, var_ready, std_ready, x_ready, transposed, xT_ready, projected, h_ready, f_done, summed, sum_start, \
        tops, maxed, args, exps, rowsT, rows_out, rows_stored, meaned, chain = (m.sem(f"{name}p_{n}") for n in (
            "loaded", "var_ready", "std_ready", "x_ready", "transposed", "xT_ready", "projected", "h_ready", "f_done",
            "summed", "sum_start", "tops", "maxed", "args", "exps", "rowsT", "rows_out", "rows_stored", "meaned",
            "chain"))
    n_loads = C + 2 + (2 if b1 is not None else 0)
    with nc.Block() as block:
        @block.sync
        def _(sp):
            for c in range(C):
                sp.dma_start(W[:, c].rearrange("p (h o) -> p h o", h=H) if H > 1 else W[:, c],
                             layer["W"][c * P:(c + 1) * P]).then_inc(loaded, 16)
            sp.dma_start(a1[:], layer["a1"].partition_broadcast(P)).then_inc(loaded, 16)
            sp.dma_start(a2[:], layer["a2"].partition_broadcast(P)).then_inc(loaded, 16)
            if b1 is not None:
                sp.dma_start(b1_wide[:], b1.partition_broadcast(P)).then_inc(loaded, 16)
                sp.dma_start(b2_wide[:], b2.partition_broadcast(P)).then_inc(loaded, 16)

            def load(t, p, is_last):
                sp.wait_ge(x_ready, t + 1)
                sp.dma_start(y_in[:, p], row_tile(m.y, t)).then_inc(y_here[p], 16)

            each_tile(sp, load)
            for q in range(PARTS):
                sp.wait_ge(rows_out, q + 1)
                heads = m.rows[q * (H // PARTS):(q + 1) * (H // PARTS)]
                sp.dma_start(heads.rearrange("h (t p) -> (h t) p", p=P), rT[0:ROWS, q]).then_inc(rows_stored, 16)
            sp.wait_ge(rows_stored, 16 * PARTS)

        @block.gpsimd
        def _(pool):
            own = Chain(pool, summed)
            nc.gpsimd.memset(h_sum[:], 0.0).then_inc(sum_start, 1)
            pool.wait_ge(sum_start, 1)

            def step(t, p, is_last):
                pool.wait_ge(h_ready, t + 3)
                own.at(t + 2)
                rows = LAST if is_last else P
                own.link(nc.gpsimd.tensor_tensor(h_sum[0:rows], h_sum[0:rows], h_out[0:rows, p], ALU.add))

            each_tile(pool, step)
            pool.wait_ge(tops, 1)
            nc.gpsimd.partition_all_reduce(f2_max[:], f2_top[:], P, RMAX).then_inc(maxed, 1)

        @block.tensor
        def _(pe):
            def transposes(t, p):
                pe.wait_ge(x_ready, t + 3)
                pe.wait_ge(xT_ready, t + 1)
                for c in range(C):
                    last = nc.tensor.transpose(pT[:, p, c * P:(c + 1) * P], x_out[:, p, c * P:(c + 1) * P], m.ident[:])
                last.then_inc(transposed, 1)

            def step(t, p, is_last):
                if not is_last:
                    transposes(t + 1, 1 - p)
                pe.wait_ge(xT_ready, t + 3)
                pe.wait_ge(h_ready, t + 1)
                for c in range(C):
                    last = nc.tensor.matmul(pH[:, p], xT[:, p, c], W[:, c], start=c == 0, stop=c == C - 1)
                last.then_inc(projected, 1)

            pe.wait_ge(loaded, 16 * n_loads)
            transposes(0, 0)
            each_tile(pe, step)
            pe.wait_ge(summed, T + 2)
            nc.tensor.matmul(pM[:], over_n[:], h_sum[:], start=True, stop=True).then_inc(meaned, 1)
            pe.wait_ge(exps, 3)
            flat = R[:].rearrange("p h t -> p (h t)")
            for q in range(PARTS):
                nc.tensor.transpose(pR[0:ROWS, q, 0:P], flat[:, q * ROWS:(q + 1) * ROWS], m.ident[:]).then_inc(rowsT, 1)

        @block.scalar
        def _(act):
            act.sem_inc(xT_ready, 2)
            act.wait_ge(var_ready, 1)
            nc.scalar.activation(work[:], work[:], ACT.Sqrt).then_inc(std_ready, 1)

            def copy_xT(t, p):
                act.wait_ge(x_ready, t + 3)
                act.dma_start(row_tile(m.x, t), x_out[:, p]).then_inc(x_stored[p], 16)
                act.wait_ge(transposed, t + 3)
                act.wait_ge(projected, t + 1)
                nc.scalar.activation(xT[:, p].rearrange("p c i -> p (c i)"), pT[:, p], ACT.Copy).then_inc(xT_ready, 1)

            def step(t, p, is_last):
                if not is_last:
                    copy_xT(t + 1, 1 - p)
                if b1 is None:
                    act.wait_ge(projected, t + 3)
                    act.wait_ge(f_done, t * 2 + 2)
                    act.wait_ge(summed, t + 1)
                    act.wait_ge(h_stored[p], (t - p) * 8 + 16)
                    nc.scalar.activation(h_out[:, p], pH[:, p], ACT.Copy).then_inc(h_ready, 1)
                act.wait_ge(h_ready, t + 3)
                act.dma_start(row_tile(m.h, t), h_out[:, p]).then_inc(h_stored[p], 16)

            copy_xT(0, 0)
            each_tile(act, step)
            for p in range(2):
                act.wait_ge(x_stored[p], 16 * (T // 2 + 1))
                act.wait_ge(h_stored[p], 16 * (T // 2 + 1))
            for n, t in enumerate((m.b, m.u, R)):
                act.wait_ge(args, n + 1)
                nc.scalar.activation(t[:, 0:H], t[:, 0:H], ACT.Exp).then_inc(exps, 1)

        @block.vector
        def _(dve):
            v = nc.vector
            own = Chain(dve, chain)
            own.link(v.memset(over_n[:], 1.0 / N))
            dve.sem_inc(x_ready, 2)
            dve.sem_inc(projected, 2)
            dve.sem_inc(transposed, 2)
            dve.sem_inc(h_ready, 2)
            dve.sem_inc(f_done, 4)
            dve.sem_inc(summed, 2)
            for p in range(2):
                dve.sem_inc(x_stored[p], 16)
                dve.sem_inc(h_stored[p], 16)

            def std(w):
                dve.sem_inc(var_ready, 1)

            load_moments(nc, dve, own, m, mean, rstd, work, std)
            dve.wait_ge(std_ready, 1)
            own.link(v.reciprocal(rstd[:], work[:]))
            dve.wait_ge(loaded, 16 * n_loads)
            before = MOMENT_LINKS + 2

            def normalise(t, p):
                dve.wait_ge(y_here[p], (t - p) * 8 + 16)
                dve.wait_ge(transposed, t + 1)
                dve.wait_ge(x_stored[p], (t - p) * 8 + 16)
                v.tensor_scalar(x_out[:, p], y_in[:, p], mean[:, bass.ts(t, 1)], rstd[:, bass.ts(t, 1)], ALU.subtract,
                                ALU.mult).then_inc(x_ready, 1)

            def step(t, p, is_last):
                if not is_last:
                    normalise(t + 1, 1 - p)
                if b1 is not None:
                    dve.wait_ge(projected, t + 3)
                    dve.wait_ge(summed, t + 1)
                    dve.wait_ge(h_stored[p], (t - p) * 8 + 16)
                    v.tensor_tensor(h_out[:, p], pH[:, p], b1_wide[:], ALU.add).then_inc(h_ready, 1)
                dve.wait_ge(h_ready, t + 3)
                own.at(t * 2 + before)
                flat = lambda a: a[:].rearrange("p h o -> p (h o)")
                dve.wait_ge(f_done, t * 2 + 4)
                own.link(v.tensor_tensor(prod[:, 0], h_out[:, p], flat(a1), ALU.mult))
                own.link(v.tensor_tensor(prod[:, 1], h_out[:, p], flat(a2), ALU.mult))
                for n, f in enumerate((f1, f2)):
                    v.tensor_reduce(f[:, :, t], prod[:, n].rearrange("p (h o) -> p h o", h=H), AX,
                                    ALU.add).then_inc(f_done, 1)

            normalise(0, 0)
            each_tile(dve, step)
            own.at(T * 2 + before)
            dve.wait_ge(f_done, 2 * T + 4)
            v.tensor_reduce(f2_top[:], f2[:], AX, ALU.max).then_inc(tops, 1)
            dve.wait_ge(maxed, 1)
            wide = lambda a: a[:].rearrange("p (h o) -> p h o", o=1).broadcast_to([P, H, T])
            own.link(v.tensor_tensor(f2[:], f2[:], wide(f2_max), ALU.subtract))
            v.tensor_scalar(m.b[:, 0:H], f2[:], B_SHIFT, None, ALU.add).then_inc(args, 1)
            v.tensor_scalar(m.u[:, 0:H], f2[:], -(1 - SLOPE), -U_SHIFT, ALU.mult, ALU.add).then_inc(args, 1)
            own.link(v.tensor_tensor(f1[:], f1[:], wide(f2_max), ALU.add))
            if b2 is not None:
                own.link(v.tensor_scalar(f1[:], f1[:], b2_wide[:], None, ALU.add))
            own.link(v.tensor_scalar(f1[:], f1[:], 1 - SLOPE, -U_SHIFT, ALU.mult, ALU.add))
            v.tensor_scalar(R[:], f1[:], R_TOP, None, ALU.min).then_inc(args, 1)
            dve.wait_ge(meaned, 1)
            v.tensor_copy(m.mean_h[:], pM[:])
            for q in range(PARTS):
                dve.wait_ge(rowsT, q + 1)
                v.tensor_copy(rT[0:ROWS, q], pR[0:ROWS, q, 0:P]).then_inc(rows_out, 1)


class Finish:

    def __init__(self, nc, sb, m, name, elu):
        self.nc, self.m, self.elu = nc, m, elu
        self.rden = sb("rden", [P, 8])
        self.share = sb("share", [P, D])
        self.neg = sb("neg", [P, D])
        self.x_in = sb("x_in", [P, 2, D])
        self.y = sb("y_out", [P, 2, D])
        self.x_here = [m.sem(f"{name}_x_here{p}") for p in range(2)]
        self.y_stored = [m.sem(f"{name}_y_stored{p}") for p in range(2)]
        self.shared, self.negated, self.exped, self.y_ready, self.acc_read, self.chain = (
            m.sem(f"{name}_{n}") for n in ("shared", "negated", "exped", "y_ready", "acc_read", "chain"))

    def start(self, dve):
        dve.sem_inc(self.y_ready, 2)
        for p in range(2):
            dve.sem_inc(self.y_stored[p], 16)
        self.own = Chain(dve, self.chain)
        self.per = 4 if self.elu else 3
        dve.sem_inc(self.acc_read, 2)

    def load_x(self, eng, t, p):
        eng.wait_ge(self.y_ready, t + 1)
        eng.dma_start(self.x_in[:, p], row_tile(self.m.x, t)).then_inc(self.x_here[p], 16)

    def store_y(self, eng, t, p):
        eng.wait_ge(self.y_ready, t + 3)
        eng.dma_start(row_tile(self.m.y, t), self.y[:, p]).then_inc(self.y_stored[p], 16)

    def all_stored(self, eng):
        for p in range(2):
            eng.wait_ge(self.y_stored[p], 16 * (T // 2 + 1))

    def exp_neg(self, act, t):
        act.wait_ge(self.shared, t + 1)
        act.wait_ge(self.y_ready, t + 2)
        self.nc.scalar.activation(self.neg[:], self.share[:], ACT.Relu, scale=-1.0).then_inc(self.negated, 1)
        act.wait_ge(self.negated, t + 1)
        self.nc.scalar.activation(self.neg[:], self.neg[:], ACT.Exp, scale=-1.0).then_inc(self.exped, 1)

    def divide(self, dve, t, den, pieces):
        v, m, own = self.nc.vector, self.m, self.own
        own.at(t * self.per)
        heads = den.shape[1]
        own.link(v.tensor_scalar(self.rden[:, 0:heads], den, m.empty[:, bass.ts(t, 1)], None, ALU.add))
        own.link(v.reciprocal(self.rden[:, 0:heads], self.rden[:, 0:heads]))
        if heads == 1:
            for to, num in pieces:
                last = v.tensor_scalar(self.share[:, to], num, self.rden[:, 0:1], None, ALU.mult)
        else:
            r = self.rden[:, 0:heads].rearrange("p (h o) -> p h o", o=1).broadcast_to([P, heads, D // heads])
            last = v.tensor_tensor(self.share[:].rearrange("p (h o) -> p h o", h=heads),
                                   pieces.rearrange("p (h o) -> p h o", h=heads), r, ALU.mult)
        last.then_inc(self.acc_read, 1)
        dve.wait_ge(self.acc_read, t + 3)
        v.scalar_tensor_tensor(out=self.share[:], in0=m.mean_h[:], scalar=m.empty[:, bass.ts(t, 1)], in1=self.share[:],
                               op0=ALU.mult, op1=ALU.add).then_inc(self.shared, 1)

    def residual(self, dve, t, p):
        v, m, own = self.nc.vector, self.m, self.own
        own.at(t * self.per + 2)
        dve.wait_ge(self.x_here[p], (t - p) * 8 + 16)
        dve.wait_ge(self.y_stored[p], (t - p) * 8 + 16)
        dve.wait_ge(self.shared, t + 1)
        if self.elu:
            dve.wait_ge(self.exped, t + 1)
            own.link(v.scalar_tensor_tensor(out=self.neg[:], in0=self.share[:], scalar=0.0, in1=self.neg[:],
                                            op0=ALU.max, op1=ALU.add))
            ins = v.scalar_tensor_tensor(out=self.y[:, p], in0=self.neg[:], scalar=-1.0, in1=self.x_in[:, p],
                                         op0=ALU.add, op1=ALU.add)
        else:
            ins = v.tensor_tensor(self.y[:, p], self.share[:], self.x_in[:, p], ALU.add)
        ins.then_inc(self.y_ready, 1)
        dve.wait_ge(self.y_ready, t + 3)
        own.link(v.bn_stats(m.stats[:, t], self.y[:, p]))


def attend_one_head(nc, ctx, m, name):
    sb = lambda n, s, d=F32: ctx.enter_context(nc.sbuf_tensor(f"{name}a_{n}", s, d))
    W = 2 * P
    CH = T // 2
    RING = 4
    LEFT = D // 2
    R = sb("R", [P, NP])
    V = sb("V", [P, T, D + 1])
    weights = sb("weights", [P, RING, W])
    acc = ctx.enter_context(nc.psum_tensor(f"{name}a_acc", [P, 2, 2, 2, BANK], F32))
    fin = Finish(nc, sb, m, name + "a", True)
    r_here, v_here, b_in, v_ready, w_ready, w_used, chunk_done = (m.sem(f"{name}a_{n}") for n in (
        "r_here", "v_here", "b_in", "v_ready", "w_ready", "w_used", "chunk_done"))

    def each_chunk(eng, first, body):
        first()
        with eng.Fori(0, (CH - 1) // 2) as pair:
            for q in range(2):
                body(pair * 2 + 1 + q, (1 + q) % 2, (1 + q) * T % RING)

    with nc.Block() as block:
        @block.sync
        def _(sp):
            sp.dma_start(R[:], m.rows[0].partition_broadcast(P)).then_inc(r_here, 16)
            h = m.h.rearrange("(t p) d -> p t d", p=P)
            for j in range(T):
                sp.dma_start(V[:, j, 0:D], h[:, j]).then_inc(v_here, 16)
            each_tile(sp, lambda t, p, is_last: fin.load_x(sp, t, p))

        @block.scalar
        def _(act):
            def fin_step(t, p, is_last):
                fin.exp_neg(act, t)
                fin.store_y(act, t, p)

            act.wait_ge(v_here, 16 * T)
            for j in range(T):
                nc.scalar.activation(V[:, j, 0:D], V[:, j, 0:D], ACT.Copy, scale=m.b[:, 0, j:j + 1]).then_inc(v_ready, 1)
            each_tile(act, fin_step)
            fin.all_stored(act)

        @block.tensor
        def _(pe):
            def chunk(c, cp, ring, first):
                for j in range(T):
                    if first:
                        pe.wait_ge(v_ready, j + 1)
                    if j == 0:
                        pe.wait_ge(fin.acc_read, c * 2)
                    pe.wait_ge(w_ready, c * T + j + 1)
                    for i in range(2):
                        w = weights[:, (ring + j) % RING, i * P:(i + 1) * P]
                        nc.tensor.matmul(acc[:, cp, i, 0, 0:D + 1 - LEFT], w, V[:, j, LEFT:D + 1],
                                         start=j == 0, stop=j == T - 1)
                        last = nc.tensor.matmul(acc[:, cp, i, 1, 0:LEFT], w, V[:, j, 0:LEFT],
                                                start=j == 0, stop=j == T - 1)
                    last.then_inc(w_used, 1)

            pe.sem_inc(w_used, RING)
            pe.wait_ge(b_in, 1)
            each_chunk(pe, lambda: chunk(0, 0, 0, True), lambda c, cp, ring: chunk(c, cp, ring, False))

        @block.vector
        def _(dve):
            v = nc.vector
            fin.start(dve)
            v.tensor_copy(V[:, :, D:D + 1].rearrange("p t o -> p (t o)"), m.b[:, 0]).then_inc(b_in, 1)
            dve.wait_ge(r_here, 16)

            def make(c, j, ring):
                dve.wait_ge(w_used, c * T + j + 1)
                v.scalar_tensor_tensor(out=weights[:, (ring + j) % RING], in0=R[:, bass.ts(c, W)],
                                       scalar=m.u[:, 0, j:j + 1], in1=m.mask[:, j, bass.ts(c, W)],
                                       op0=ALU.max, op1=ALU.mult).then_inc(w_ready, 1)

            def divide(c, cp, i):
                dve.wait_ge(w_used, (c + 1) * T + RING)
                a = acc[:, cp, i]
                fin.divide(dve, c * 2 + i, a[:, 0, D - LEFT:D - LEFT + 1],
                           [(slice(0, LEFT), a[:, 1, 0:LEFT]), (slice(LEFT, D), a[:, 0, 0:D - LEFT])])

            def first():
                for j in range(T):
                    make(0, j, 0)

            def chunk(c, cp, ring):
                for j in range(T):
                    make(c, j, ring)
                    if j in (4, 14):
                        divide(c - 1, 1 - cp, (j - 4) // 10)
                    if j in (8, 18):
                        i = (j - 8) // 10
                        fin.residual(dve, (c - 1) * 2 + i, i)

            each_chunk(dve, first, chunk)
            for i in range(2):
                divide(CH - 1, (CH - 1) % 2, i)
                fin.residual(dve, (CH - 1) * 2 + i, i)


def attend_heads(nc, ctx, m, name, H):
    O = D // H
    sb = lambda n, s, d=F32: ctx.enter_context(nc.sbuf_tensor(f"{name}a_{n}", s, d))
    R = sb("R", [P, 2, NP])
    V = sb("V", [P, 2, T, O + 1])
    weights = sb("weights", [P, 2, NP])
    sums = sb("sums", [P, NP])
    BANKS = -(-NP // BANK)
    acc = ctx.enter_context(nc.psum_tensor(f"{name}a_acc", [P, BANKS, BANK], F32))
    width = [min(BANK, NP - k * BANK) for k in range(BANKS)]
    r_here = [m.sem(f"{name}a_r_here{p}") for p in range(2)]
    v_here = [m.sem(f"{name}a_v_here{p}") for p in range(2)]
    v_scaled, v_ready, w_ready, w_used, bank_done, evacuated, stored = (m.sem(f"{name}a_{n}") for n in (
        "v_scaled", "v_ready", "w_ready", "w_used", "bank_done", "evacuated", "stored"))

    def each_head(eng, body):
        with eng.Fori(0, H // 2) as pair:
            for p in range(2):
                body(pair * 2 + p, p)

    with nc.Block() as block:
        @block.sync
        def _(sp):
            values = m.h.rearrange("(t p) (h o) -> h p t o", p=P, h=H)

            def load(h, p):
                sp.wait_ge(w_ready, (h + 1) * T)
                sp.dma_start(R[:, p], m.rows[h].partition_broadcast(P)).then_inc(r_here[p], 16)
                sp.wait_ge(w_used, (h + 1) * T)
                sp.dma_start(V[:, p, :, 0:O], values[h]).then_inc(v_here[p], 16)

            each_head(sp, load)

        @block.gpsimd
        def _(pool):
            def scale(h, p):
                pool.wait_ge(v_here[p], (h - p) * 8 + 16)
                b = m.b[:, h].rearrange("p (t o) -> p t o", o=1)
                nc.gpsimd.tensor_tensor(V[:, p, :, 0:O], V[:, p, :, 0:O], b.broadcast_to([P, T, O]),
                                        ALU.mult).then_inc(v_ready, 1)
                nc.gpsimd.tensor_copy(V[:, p, :, O:O + 1], b).then_inc(v_ready, 1)

            each_head(pool, scale)

        @block.vector
        def _(dve):
            dve.sem_inc(w_ready, 2 * T)

            def head(h, p):
                dve.wait_ge(r_here[p], (h - p) * 8 + 16)
                for j in range(T):
                    dve.wait_ge(w_used, (h + 2) * T + j - 1)
                    nc.vector.scalar_tensor_tensor(out=weights[:, j % 2], in0=R[:, p], scalar=m.u[:, h, j:j + 1],
                                                   in1=m.mask[:, j], op0=ALU.max, op1=ALU.mult).then_inc(w_ready, 1)

            each_head(dve, head)

        @block.tensor
        def _(pe):
            pe.sem_inc(w_used, 2 * T)

            def head(h, p):
                pe.wait_ge(v_ready, (h + 1) * 2)
                for j in range(T):
                    pe.wait_ge(w_ready, (h + 2) * T + j + 1)
                    for k in range(BANKS):
                        if j == 0:
                            pe.wait_ge(evacuated, h * BANKS + k + 1)
                        last = nc.tensor.matmul(acc[0:O + 1, k, 0:width[k]], V[:, p, j],
                                                weights[:, j % 2, k * BANK:k * BANK + width[k]],
                                                start=j == 0, stop=j == T - 1)
                        if j == T - 1 and k < BANKS - 1:
                            last.then_inc(bank_done, 1)
                    last.then_inc(w_used, 1)

            each_head(pe, head)

        @block.scalar
        def _(act):
            act.sem_inc(evacuated, BANKS)
            act.sem_inc(stored, 32)

            def head(h, p):
                act.wait_ge(stored, h * 32 + 32)
                for k in range(BANKS):
                    if k < BANKS - 1:
                        act.wait_ge(bank_done, h * (BANKS - 1) + k + 1)
                    else:
                        act.wait_ge(w_used, (h + 3) * T)
                    nc.scalar.activation(sums[0:O + 1, k * BANK:k * BANK + width[k]], acc[0:O + 1, k, 0:width[k]],
                                         ACT.Copy).then_inc(evacuated, 1)
                act.wait_ge(evacuated, (h + 2) * BANKS)
                act.dma_start(m.num[h], sums[0:O]).then_inc(stored, 16)
                act.dma_start(m.den[bass.ts(h, 1)], sums[O:O + 1]).then_inc(stored, 16)

            each_head(act, head)
            act.wait_ge(stored, H * 32 + 32)


def finish_heads(nc, ctx, m, name, H, elu):
    O = D // H
    sb = lambda n, s, d=F32: ctx.enter_context(nc.sbuf_tensor(f"{name}f_{n}", s, d))
    num = sb("num", [P, 2, C, P])
    den = sb("den", [H, 2, P])
    pN = ctx.enter_context(nc.psum_tensor(f"{name}f_pN", [P, 2, BANK], F32))
    pD = ctx.enter_context(nc.psum_tensor(f"{name}f_pD", [P, 2, BANK], F32))
    fin = Finish(nc, sb, m, name + "f", elu)
    here = [m.sem(f"{name}f_here{p}") for p in range(2)]
    turned = m.sem(f"{name}f_turned")
    with nc.Block() as block:
        @block.sync
        def _(sp):
            pairs = m.num.rearrange("(c a) o n -> (a o) c n", a=P // O)

            def load(t, p, is_last):
                sp.wait_ge(turned, t + 1)
                sp.dma_start(num[:, p], pairs[:, :, bass.ts(t, P)]).then_inc(here[p], 16)
                sp.dma_start(den[:, p], m.den[0:H, bass.ts(t, P)]).then_inc(here[p], 16)
                fin.load_x(sp, t, p)

            each_tile(sp, load)

        @block.tensor
        def _(pe):
            pe.sem_inc(turned, 2)

            def turn(t, p, is_last):
                pe.wait_ge(here[p], (t - p) * 16 + 32)
                pe.wait_ge(fin.acc_read, t + 1)
                for c in range(C):
                    nc.tensor.transpose(pN[:, p, c * P:(c + 1) * P], num[:, p, c], m.ident[:])
                nc.tensor.transpose(pD[:, p, 0:H], den[:, p], m.ident[0:H, 0:H]).then_inc(turned, 1)

            each_tile(pe, turn)

        @block.scalar
        def _(act):
            def step(t, p, is_last):
                if elu:
                    fin.exp_neg(act, t)
                fin.store_y(act, t, p)

            each_tile(act, step)
            fin.all_stored(act)

        @block.vector
        def _(dve):
            fin.start(dve)

            def step(t, p, is_last):
                dve.wait_ge(turned, t + 3)
                fin.divide(dve, t, pD[:, p, 0:H], pN[:, p])
                fin.residual(dve, t, p)

            each_tile(dve, step)


def normalise_out(nc, ctx, m, out):
    sb = lambda n, s, d=F32: ctx.enter_context(nc.sbuf_tensor("no_" + n, s, d))
    y_in, x_out = sb("y", [P, 2, D]), sb("x", [P, 2, D])
    mean, rstd, work = sb("mean", [P, T]), sb("rstd", [P, T]), sb("work", [P, T])
    y_here = [m.sem(f"no_y_here{p}") for p in range(2)]
    stored = [m.sem(f"no_stored{p}") for p in range(2)]
    var_ready, std_ready, x_ready, chain = (m.sem("no_" + n) for n in ("var_ready", "std_ready", "x_ready", "chain"))
    with nc.Block() as block:
        @block.sync
        def _(sp):
            def load(t, p, is_last):
                sp.wait_ge(x_ready, t + 1)
                sp.dma_start(y_in[:, p], row_tile(m.y, t)).then_inc(y_here[p], 16)

            each_tile(sp, load)

        @block.scalar
        def _(act):
            act.wait_ge(var_ready, 1)
            nc.scalar.activation(work[:], work[:], ACT.Sqrt).then_inc(std_ready, 1)

            def store(t, p, is_last):
                act.wait_ge(x_ready, t + 3)
                if is_last:
                    act.dma_start(out[(T - 1) * P:N], x_out[0:LAST, p]).then_inc(stored[p], 16)
                else:
                    act.dma_start(out[0:(T - 1) * P].rearrange("(t p) d -> t p d", p=P)[t],
                                  x_out[:, p]).then_inc(stored[p], 16)

            each_tile(act, store)
            for p in range(2):
                act.wait_ge(stored[p], 16 * (T // 2 + 1))

        @block.vector
        def _(dve):
            own = Chain(dve, chain)
            dve.sem_inc(x_ready, 2)
            for p in range(2):
                dve.sem_inc(stored[p], 16)
            load_moments(nc, dve, own, m, mean, rstd, work, lambda w: dve.sem_inc(var_ready, 1))
            dve.wait_ge(std_ready, 1)
            own.link(nc.vector.reciprocal(rstd[:], work[:]))

            def step(t, p, is_last):
                dve.wait_ge(y_here[p], (t - p) * 8 + 16)
                dve.wait_ge(stored[p], (t - p) * 8 + 16)
                nc.vector.tensor_scalar(x_out[:, p], y_in[:, p], mean[:, bass.ts(t, 1)], rstd[:, bass.ts(t, 1)], ALU.subtract,
                                        ALU.mult).then_inc(x_ready, 1)

            each_tile(dve, step)


_INS = ["x", "adj", "L0_gnn_W_self", "L0_gnn_b_self", "L0_gnn_W_nb", "L0_gnn_b_nb", "L0_gnn_W_comb", "L0_gnn_b_comb",
        "L1_gnn_W1", "L1_gnn_b1", "L1_gnn_a1", "L1_gnn_a2", "L1_gnn_b2", "L2_gnn_W", "L2_gnn_a1", "L2_gnn_a2",
        "L3_gnn_W", "L3_gnn_a"]


def kernel(**inputs):
    import numpy as _np
    import concourse.bacc as _bacc
    from concourse import mybir as _mybir
    from concourse.bass_utils import run_bass_kernel_spmd as _run

    nc = _bacc.Bacc("TRN2", target_bir_lowering=False, num_devices=1)
    arrays, args = {}, []
    for name in _INS:
        a = _np.ascontiguousarray(inputs[name]).reshape(_np.shape(inputs[name]) or (1,))
        arrays[f"in_{name}"] = a
        args.append(nc.dram_tensor(f"in_{name}", a.shape, _mybir.dt.from_np(a.dtype), kind="ExternalInput").ap())
    out = nc.dram_tensor("out", (N, D), F32, kind="ExternalOutput").ap()
    gnn_kernel(nc, *args, out)
    r = _run(nc, [arrays], core_ids=[0])
    return r.results[0]["out"]
```

```python
from contextlib import ExitStack

import concourse.bass as bass
from concourse import mybir

ALU = mybir.AluOpType
ACT = mybir.ActivationFunctionType
AX = mybir.AxisListType.X
F32 = mybir.dt.float32
BF16 = mybir.dt.bfloat16
F32R = mybir.dt.float32r
I32 = mybir.dt.int32
U8 = mybir.dt.uint8
RMAX = bass.bass_isa.ReduceOp.max

P = 128
BANK = 512
N = 3327
T = -(-N // P)
NP = T * P
LAST = N - (T - 1) * P
D = 512
C = D // P
SLOPE = 0.2
EPS = 1e-5
B_SHIFT = 30.0
U_SHIFT = 60.0
R_TOP = 45.0


class Chain:

    def __init__(self, eng, sem):
        self.eng, self.sem, self.base, self.n = eng, sem, 0, 0

    def at(self, base):
        self.base, self.n = base, 0

    def link(self, ins):
        ins.then_inc(self.sem, 1)
        self.n += 1
        self.eng.wait_ge(self.sem, self.base + self.n)


def each_tile(eng, step):
    with eng.Fori(0, T // 2 - 1) as pair:
        for p in range(2):
            step(pair * 2 + p, p, 2)
    for p in range(2):
        step(T - 2 + p, p, 1 - p)


def row_tile(dram, t):
    return dram.rearrange("(t p) d -> t p d", p=P)[t]


def gnn_kernel(nc, x, adj, L0_gnn_W_self, L0_gnn_b_self, L0_gnn_W_nb, L0_gnn_b_nb, L0_gnn_W_comb, L0_gnn_b_comb,
               L1_gnn_W1, L1_gnn_b1, L1_gnn_a1, L1_gnn_a2, L1_gnn_b2, L2_gnn_W, L2_gnn_a1, L2_gnn_a2,
               L3_gnn_W, L3_gnn_a, out):
    with ExitStack() as ctx:
        m = Memory(nc, ctx)
        with ExitStack() as first:
            m.zs = first.enter_context(nc.sbuf_tensor("zs", [P, T, 3, D], BF16))
            with ExitStack() as s:
                fold_weights(nc, s, m, L0_gnn_W_self, L0_gnn_b_self, L0_gnn_W_nb, L0_gnn_b_nb,
                             L0_gnn_W_comb, L0_gnn_b_comb)
                m.end_stage()
                project_input(nc, s, m, x)
            m.end_stage()
            with ExitStack() as s:
                aggregate(nc, s, m, x, adj)
            m.end_stage()
        m.attention_state(nc, ctx)
        head = lambda w: w.rearrange("h d o -> d h o")
        layers = [
            dict(H=1, W=L1_gnn_W1, a1=L1_gnn_a1.rearrange("(h o) -> h o", h=1),
                 a2=L1_gnn_a2.rearrange("(h o) -> h o", h=1), b1=L1_gnn_b1, b2=L1_gnn_b2, elu=True),
            dict(H=8, W=head(L2_gnn_W), a1=L2_gnn_a1, a2=L2_gnn_a2, b1=None, b2=None, elu=True),
            dict(H=8, W=head(L3_gnn_W), a1=L3_gnn_a[:, 0:64], a2=L3_gnn_a[:, 64:128], b1=None, b2=None, elu=False),
        ]
        for n, layer in enumerate(layers, 1):
            with ExitStack() as s:
                project(nc, s, m, f"L{n}", layer)
            m.end_stage()
            with ExitStack() as s:
                if layer["H"] == 1:
                    attend_one_head(nc, s, m, f"L{n}")
                else:
                    attend_heads(nc, s, m, f"L{n}", layer["H"])
            m.end_stage()
            if layer["H"] > 1:
                with ExitStack() as s:
                    finish_heads(nc, s, m, f"L{n}", layer["H"], layer["elu"], out if n == len(layers) else None)
                m.end_stage()


class Memory:

    def __init__(self, nc, ctx):
        sb = lambda n, s, d: ctx.enter_context(nc.sbuf_tensor(n, s, d))
        dram = lambda n, s: nc.dram_tensor(n, s, F32, kind="Internal").ap()
        self.mask = sb("mask", [P, T, NP], U8)
        self.ident = sb("ident", [P, P], F32)
        self.identb = sb("identb", [P, P], BF16)
        self.empty = sb("empty", [P, T], F32)
        self.stats = sb("stats", [P, T, 6], F32)
        self.y = dram("y_scratch", [NP, D])
        self.x = dram("x_scratch", [NP, D])
        self.self_part = dram("self_scratch", [NP, D])
        self.h = dram("h_scratch", [NP, D])
        self.rows = dram("r_scratch", [8, NP])
        self.num = dram("num_scratch", [T, 8, 64, P])
        self.den = dram("den_scratch", [T, 8, P])
        self.nc, self.stage_sems = nc, []

    def sem(self, name):
        self.stage_sems.append(self.nc.alloc_semaphore(name=name))
        return self.stage_sems[-1]

    def end_stage(self):
        self.nc.clear_and_free_semaphores(self.stage_sems)
        self.stage_sems = []
        self.nc.all_engine_barrier()

    def attention_state(self, nc, ctx):
        sb = lambda n, s, d: ctx.enter_context(nc.sbuf_tensor(n, s, d))
        self.u = sb("u", [P, 8, T], F32)
        self.b = sb("b", [P, 8, T], F32)
        self.mean_h = sb("mean_h", [P, D], F32)


def fold_weights(nc, ctx, m, w_self, b_self, w_nb, b_nb, w_comb, b_comb):
    sb = lambda n, s, d=F32: ctx.enter_context(nc.sbuf_tensor(n, s, d))
    m.fold = sb("fold", [P, 2, C, D])
    m.fold_bias = sb("fold_bias", [P, D])
    with ExitStack() as s2:
        sb = lambda n, s, d=F32: s2.enter_context(nc.sbuf_tensor(n, s, d))
        ps = lambda n, s: s2.enter_context(nc.psum_tensor(n, s, F32))
        space = m.zs[:].rearrange("p t s d -> p (t s d)").bitcast(F32)
        size = 2 * C * D
        w_in, wT, wc = (space[:, n * size:(n + 1) * size].rearrange("p (w c n) -> p w c n", w=2, c=C) for n in range(3))
        bias_col = sb("bias_col", [P, 2, C])
        bias_wide = sb("bias_wide", [P, 2, C, P])
        bias_comb = sb("bias_comb", [P, D])
        ones = sb("ones_row", [P, P])
        pT = ps("pT", [P, 2, BANK])
        pF = ps("pF", [P, 2, BANK])
        pB = ps("pB", [P, BANK])
        loaded, zeroed, ident_ready, wide, transposed, copied, product, product_used, bias_done, done = (
            m.sem("fw_" + n) for n in ("loaded", "zeroed", "ident", "wide", "transposed", "copied", "product",
                                       "product_used", "bias_done", "done"))
        with nc.Block() as block:
            @block.sync
            def _(sp):
                sp.dma_start(w_in[:, 0], w_self.rearrange("(c p) n -> p c n", p=P)).then_inc(loaded, 16)
                sp.dma_start(w_in[:, 1], w_nb.rearrange("(c p) n -> p c n", p=P)).then_inc(loaded, 16)
                sp.dma_start(wc[:, 0], w_comb[0:D].rearrange("(c p) n -> p c n", p=P)).then_inc(loaded, 16)
                sp.dma_start(wc[:, 1], w_comb[D:2 * D].rearrange("(c p) n -> p c n", p=P)).then_inc(loaded, 16)
                with nc.allow_non_contiguous_dma("two small bias columns"):
                    sp.dma_start(bias_col[:, 0], b_self.rearrange("(c p) -> p c", p=P)).then_inc(loaded, 16)
                    sp.dma_start(bias_col[:, 1], b_nb.rearrange("(c p) -> p c", p=P)).then_inc(loaded, 16)
                sp.dma_start(bias_comb[:], b_comb.partition_broadcast(P)).then_inc(loaded, 16)
                sp.wait_ge(loaded, 7 * 16)

            @block.gpsimd
            def _(pool):
                nc.gpsimd.memset(m.ident[:], 0.0).then_inc(zeroed, 1)
                nc.gpsimd.memset(m.identb[:], 0.0).then_inc(zeroed, 1)
                pool.wait_ge(zeroed, 2)
                for t in (m.ident, m.identb):
                    nc.gpsimd.affine_select(out=t[:], in_=t[:], compare_op=ALU.not_equal, fill=1.0, base=0,
                                            pattern=[[-1, P]], channel_multiplier=1).then_inc(ident_ready, 1)

            @block.vector
            def _(dve):
                nc.vector.memset(ones[:], 1.0).then_inc(wide, 1)
                dve.wait_ge(wide, 1)
                dve.wait_ge(loaded, 7 * 16)
                for w in range(2):
                    for c in range(C):
                        nc.vector.tensor_scalar(bias_wide[:, w, c], ones[:], bias_col[:, w, c:c + 1], None,
                                                ALU.mult).then_inc(wide, 1)
                for n in range(2 * C):
                    dve.wait_ge(product, n + 1)
                    nc.vector.tensor_copy(m.fold[:, n // C, n % C], pF[:, n % 2]).then_inc(product_used, 1)
                dve.wait_ge(bias_done, 1)
                nc.vector.tensor_tensor(m.fold_bias[:], pB[:], bias_comb[:], ALU.add).then_inc(done, 1)

            @block.scalar
            def _(act):
                for n in range(2 * C):
                    act.wait_ge(transposed, n + 1)
                    nc.scalar.activation(wT[:, n // C, n % C], pT[:, n % 2], ACT.Copy).then_inc(copied, 1)

            @block.tensor
            def _(pe):
                pe.wait_ge(ident_ready, 2)
                pe.wait_ge(loaded, 7 * 16)
                for n in range(2 * C):
                    w, c = n // C, n % C
                    if n >= 2:
                        pe.wait_ge(copied, n - 1)
                    for k in range(C):
                        last = nc.tensor.transpose(pT[:, n % 2, k * P:(k + 1) * P],
                                                   w_in[:, w, k, c * P:(c + 1) * P], m.ident[:])
                    last.then_inc(transposed, 1)
                pe.wait_ge(copied, 2 * C)
                for n in range(2 * C):
                    w, k = n // C, n % C
                    if n >= 2:
                        pe.wait_ge(product_used, n - 1)
                    for c in range(C):
                        last = nc.tensor.matmul(pF[:, n % 2], wT[:, w, c, k * P:(k + 1) * P], wc[:, w, c],
                                                start=c == 0, stop=c == C - 1)
                    last.then_inc(product, 1)
                pe.wait_ge(wide, 2 * C + 1)
                for n in range(2 * C):
                    last = nc.tensor.matmul(pB[:], bias_wide[:, n // C, n % C], wc[:, n // C, n % C],
                                            start=n == 0, stop=n == 2 * C - 1)
                last.then_inc(bias_done, 1)


def project_input(nc, ctx, m, x):
    sb = lambda n, s, d=F32: ctx.enter_context(nc.sbuf_tensor(n, s, d))
    ps = lambda n, s: ctx.enter_context(nc.psum_tensor(n, s, F32))
    x_in = sb("pi_x", [P, 2, D])
    xT = sb("pi_xT", [P, 2, C, P])
    self_out = sb("pi_self", [P, 2, D])
    rest = sb("pi_rest", [P, 2, D])
    pT, pS, pZ = ps("pi_pT", [P, 2, BANK]), ps("pi_pS", [P, 2, BANK]), ps("pi_pZ", [P, 2, BANK])
    x_here = [m.sem(f"pi_x_here{p}") for p in range(2)]
    stored = [m.sem(f"pi_stored{p}") for p in range(2)]
    cleared, transposed, xT_ready, self_ready, self_made, z_ready, z_top, pZ_read, chain = (
        m.sem("pi_" + n) for n in ("cleared", "transposed", "xT_ready", "self_ready", "self_made", "z_ready", "z_top",
                                   "pZ_read", "chain"))
    with nc.Block() as block:
        @block.sync
        def _(sp):
            sp.wait_ge(cleared, 1)

            def load(t, p, left):
                sp.wait_ge(transposed, t + 1)
                if not left:
                    sp.dma_start(x_in[0:LAST, p], x[(T - 1) * P:N]).then_inc(x_here[p], 16)
                else:
                    full = x[0:(T - 1) * P].rearrange("(t p) d -> t p d", p=P)
                    sp.dma_start(x_in[:, p], full[t]).then_inc(x_here[p], 16)

            each_tile(sp, load)

        @block.gpsimd
        def _(pool):
            nc.gpsimd.memset(x_in[:], 0.0).then_inc(cleared, 1)

        @block.tensor
        def _(pe):
            def transposes(t, p):
                pe.wait_ge(x_here[p], (t - p) * 8 + 16)
                pe.wait_ge(xT_ready, t + 1)
                for c in range(C):
                    last = nc.tensor.transpose(pT[:, p, c * P:(c + 1) * P], x_in[:, p, c * P:(c + 1) * P], m.ident[:])
                last.then_inc(transposed, 1)

            def products(t, p, left):
                if left:
                    transposes(t + 1, 1 - p)
                pe.wait_ge(xT_ready, t + 3)
                pe.wait_ge(self_made, t + 1)
                for c in range(C):
                    last = nc.tensor.matmul(pS[:, p], xT[:, p, c], m.fold[:, 0, c], start=c == 0, stop=c == C - 1)
                last.then_inc(self_ready, 1)
                pe.wait_ge(pZ_read, t + 1)
                for c in range(C):
                    last = nc.tensor.matmul(pZ[:, p], xT[:, p, c], m.fold[:, 1, c], start=c == 0, stop=c == C - 1)
                last.then_inc(z_ready, 1)

            pe.sem_inc(transposed, 2)
            pe.sem_inc(z_ready, 2)
            transposes(0, 0)
            each_tile(pe, products)

        @block.scalar
        def _(act):
            act.sem_inc(xT_ready, 2)

            def copy_xT(t, p):
                act.wait_ge(transposed, t + 3)
                act.wait_ge(z_ready, t + 1)
                nc.scalar.activation(xT[:, p].rearrange("p c i -> p (c i)"), pT[:, p], ACT.Copy).then_inc(xT_ready, 1)

            def step(t, p, left):
                if left:
                    copy_xT(t + 1, 1 - p)
                act.wait_ge(z_ready, t + 3)
                nc.scalar.activation(m.zs[:, t, 0], pZ[:, p], ACT.Copy).then_inc(z_top, 1)
                act.wait_ge(self_made, t + 3)
                act.dma_start(row_tile(m.self_part, t), self_out[:, p]).then_inc(stored[p], 16)

            copy_xT(0, 0)
            each_tile(act, step)
            for p in range(2):
                act.wait_ge(stored[p], 16 * (T // 2 + 1))

        @block.vector
        def _(dve):
            dve.sem_inc(self_made, 2)
            dve.sem_inc(pZ_read, 2)
            for p in range(2):
                dve.sem_inc(stored[p], 16)
            own = Chain(dve, chain)

            def step(t, p, left):
                own.at(t)
                dve.wait_ge(self_ready, t + 1)
                dve.wait_ge(stored[p], (t - p) * 8 + 16)
                nc.vector.tensor_tensor(self_out[:, p], pS[:, p], m.fold_bias[:], ALU.add).then_inc(self_made, 1)
                dve.wait_ge(z_top, t + 1)
                nc.vector.tensor_tensor(rest[:, p], pZ[:, p], m.zs[:, t, 0], ALU.subtract).then_inc(pZ_read, 1)
                dve.wait_ge(pZ_read, t + 3)
                own.link(nc.vector.tensor_copy(m.zs[:, t, 1], rest[:, p]))
                nc.vector.tensor_tensor(m.zs[:, t, 2], rest[:, p], m.zs[:, t, 1], ALU.subtract)

            each_tile(dve, step)


def aggregate(nc, ctx, m, x, adj):
    sb = lambda n, s, d=F32: ctx.enter_context(nc.sbuf_tensor(n, s, d))
    HALF = NP // 2
    GROUP = 8
    GROUPS = -(-T // GROUP)
    adj_in = sb("ag_adj", [P, 2, HALF], I32)
    masked = sb("ag_masked", [P, NP], BF16)
    maskT = sb("ag_maskT", [P, 2, T, P], BF16)
    x_in = sb("ag_x", [P, D])
    self_in = sb("ag_self", [P, D])
    y = sb("ag_y", [P, D])
    degree = sb("ag_degree", [P, T, 2])
    small = sb("ag_small", [P, 2])
    part = sb("ag_part", [P, D])
    pT = ctx.enter_context(nc.psum_tensor("ag_pT", [P, GROUPS, GROUP, P], BF16))
    pA = ctx.enter_context(nc.psum_tensor("ag_pA", [P, 2, BANK], F32))
    adj_here = [m.sem(f"ag_adj_here{h}") for h in range(2)]
    cleared, adj_masked, transposed, maskT_ready, stored_mask, aggregated, pA_read, rows_here, rows_used, y_ready, \
        y_stored, chain = (m.sem("ag_" + n) for n in (
            "cleared", "adj_masked", "transposed", "maskT_ready", "stored_mask", "aggregated", "pA_read", "rows_here",
            "rows_used", "y_ready", "y_stored", "chain"))
    with nc.Block() as block:
        @block.sync
        def _(sp):
            sp.wait_ge(cleared, 2)

            def load(t, p, left):
                for h in range(2):
                    cols = HALF if h == 0 else N - HALF
                    sp.wait_ge(adj_masked, t * 2 + h + 1)
                    if not left:
                        sp.dma_start(adj_in[0:LAST, h, 0:cols], adj[(T - 1) * P:N, h * HALF:h * HALF + cols])\
                          .then_inc(adj_here[h], 16)
                    else:
                        full = adj[0:(T - 1) * P].rearrange("(t p) j -> t p j", p=P)
                        sp.dma_start(adj_in[:, h, 0:cols], full[t][:, h * HALF:h * HALF + cols])\
                          .then_inc(adj_here[h], 16)

            each_tile(sp, load)

        @block.gpsimd
        def _(pool):
            pool.memset(x_in[:], 0.0).then_inc(cleared, 1)

            def step(t, p, left):
                pool.wait_ge(maskT_ready, (t + 2) * GROUPS)
                nc.gpsimd.tensor_copy(m.mask[:, :, bass.ts(t, P)], maskT[:, p]).then_inc(stored_mask, 1)

            pool.sem_inc(stored_mask, 2)
            each_tile(pool, step)

        @block.scalar
        def _(act):
            act.wait_ge(cleared, 2)

            def rows(t, left):
                act.wait_ge(rows_used, t + 1)
                if not left:
                    act.dma_start(x_in[0:LAST], x[(T - 1) * P:N]).then_inc(rows_here, 16)
                else:
                    full = x[0:(T - 1) * P].rearrange("(t p) d -> t p d", p=P)
                    act.dma_start(x_in[:], full[t]).then_inc(rows_here, 16)
                act.dma_start(self_in[:], row_tile(m.self_part, t)).then_inc(rows_here, 16)

            def copies(t, p):
                act.wait_ge(aggregated, t + 1)
                act.wait_ge(stored_mask, t + 1)
                for g in range(GROUPS):
                    k = min(GROUP, T - g * GROUP)
                    act.wait_ge(transposed, t * GROUPS + g + 1)
                    nc.scalar.activation(maskT[:, p, g * GROUP:g * GROUP + k], pT[:, g, 0:k],
                                         ACT.Copy).then_inc(maskT_ready, 1)

            def step(t, p, left):
                rows(t, left)
                if left:
                    copies(t + 1, 1 - p)
                act.wait_ge(y_ready, t + 1)
                act.dma_start(row_tile(m.y, t), y[:]).then_inc(y_stored, 16)

            act.sem_inc(maskT_ready, GROUPS)
            copies(0, 0)
            each_tile(act, step)
            act.wait_ge(y_stored, 16 * (T + 1))

        @block.tensor
        def _(pe):
            def transposes(t, p):
                for g in range(GROUPS):
                    k = min(GROUP, T - g * GROUP)
                    if g == 0:
                        pe.wait_ge(adj_masked, t * 2 + 4)
                    pe.wait_ge(maskT_ready, t * GROUPS + g + 1)
                    for c in range(k):
                        last = nc.tensor.transpose(pT[:, g, c], masked[:, bass.ts(g * GROUP + c, P)], m.identb[:])
                    last.then_inc(transposed, 1)

            def step(t, p, left):
                if left:
                    transposes(t + 1, 1 - p)
                pe.wait_ge(maskT_ready, (t + 2) * GROUPS)
                pe.wait_ge(pA_read, t + 1)
                for j in range(T):
                    for part in range(3):
                        last = nc.tensor.matmul(pA[:, p], maskT[:, p, j], m.zs[:, j, part],
                                                start=j == 0 and part == 0, stop=j == T - 1 and part == 2)
                last.then_inc(aggregated, 1)

            pe.sem_inc(aggregated, 2)
            transposes(0, 0)
            each_tile(pe, step)

        @block.vector
        def _(dve):
            own = Chain(dve, chain)
            nc.vector.memset(adj_in[:], 0).then_inc(cleared, 1)
            dve.sem_inc(adj_masked, 2)
            dve.sem_inc(pA_read, 2)
            dve.sem_inc(rows_used, 1)
            dve.sem_inc(y_stored, 16)

            def mask_rows(t):
                if not isinstance(t, int) or t > 0:
                    dve.wait_ge(transposed, t * GROUPS)
                for h in range(2):
                    dve.wait_ge(adj_here[h], (t + 1) * 16)
                    nc.vector.tensor_scalar(masked[:, h * HALF:(h + 1) * HALF], adj_in[:, h], 0.0, 0.0, ALU.is_gt,
                                            ALU.add, accum_out=degree[:, t, h:h + 1]).then_inc(adj_masked, 1)

            def step(t, p, left):
                if left >= 2:
                    mask_rows(t + 2)
                own.at(t * 5)
                dve.wait_ge(adj_masked, t * 2 + 4)
                own.link(nc.vector.tensor_tensor(small[:, 0:1], degree[:, t, 0:1], degree[:, t, 1:2], ALU.add))
                own.link(nc.vector.tensor_scalar(m.empty[:, bass.ts(t, 1)], small[:, 0:1], 0.0, None, ALU.is_equal))
                own.link(nc.vector.tensor_scalar(small[:, 0:1], small[:, 0:1], 1.0, None, ALU.max))
                own.link(nc.vector.reciprocal(small[:, 1:2], small[:, 0:1]))
                dve.wait_ge(aggregated, t + 3)
                dve.wait_ge(rows_here, (t + 1) * 32)
                nc.vector.scalar_tensor_tensor(out=part[:], in0=pA[:, p], scalar=small[:, 1:2], in1=self_in[:],
                                               op0=ALU.mult, op1=ALU.add).then_inc(pA_read, 1)
                dve.wait_ge(pA_read, t + 3)
                dve.wait_ge(y_stored, (t + 1) * 16)
                nc.vector.scalar_tensor_tensor(out=y[:], in0=part[:], scalar=0.0, in1=x_in[:],
                                               op0=ALU.max, op1=ALU.add).then_inc(y_ready, 1)
                dve.wait_ge(y_ready, t + 1)
                dve.sem_inc(rows_used, 1)
                own.link(nc.vector.bn_stats(m.stats[:, t], y[:]))

            mask_rows(0)
            mask_rows(1)
            each_tile(dve, step)


def load_moments(nc, dve, own, m, mean, rstd, work, std_ready):
    st = m.stats
    v = nc.vector
    own.link(v.tensor_tensor(mean[:], st[:, :, 1], st[:, :, 4], ALU.add))
    own.link(v.tensor_tensor(work[:], st[:, :, 1], st[:, :, 4], ALU.subtract))
    own.link(v.tensor_scalar(mean[:], mean[:], 0.5, None, ALU.mult))
    own.link(v.tensor_scalar(work[:], work[:], 0.5, None, ALU.mult))
    own.link(v.tensor_tensor(work[:], work[:], work[:], ALU.mult))
    own.link(v.tensor_tensor(rstd[:], st[:, :, 2], st[:, :, 5], ALU.add))
    own.link(v.tensor_scalar(rstd[:], rstd[:], 1.0 / D, EPS, ALU.mult, ALU.add))
    own.link(v.tensor_tensor(work[:], work[:], rstd[:], ALU.add))
    std_ready(work)


MOMENT_LINKS = 8


def project(nc, ctx, m, name, layer):
    H, b1, b2 = layer["H"], layer["b1"], layer["b2"]
    O = D // H
    PARTS = 2 if H > 1 else 1
    ROWS = H * T // PARTS
    sb = lambda n, s, d=F32: ctx.enter_context(nc.sbuf_tensor(f"{name}p_{n}", s, d))
    ps = lambda n, s: ctx.enter_context(nc.psum_tensor(f"{name}p_{n}", s, F32))
    W = sb("W", [P, C, D])
    a1, a2 = sb("a1", [P, H, O]), sb("a2", [P, H, O])
    b1_wide = sb("b1", [P, D])
    b2_wide = sb("b2", [P, 1])
    y_in, x_out = sb("y", [P, 2, D]), sb("x", [P, 2, D])
    xT = sb("xT", [P, 2, C, P])
    h_out = sb("h", [P, 2, D])
    prod = sb("prod", [P, 2, D])
    h_sum = sb("h_sum", [P, D])
    f1, f2, R = sb("f1", [P, H, T]), sb("f2", [P, H, T]), sb("R", [P, H, T])
    f2_top, f2_max = sb("f2_top", [P, H]), sb("f2_max", [P, H])
    mean, rstd, shift, work = (sb(n, [P, T]) for n in ("mean", "rstd", "shift", "work"))
    over_n = sb("over_n", [P, P])
    rT = sb("rT", [P, 2, P])
    pT, pH = ps("pT", [P, 2, BANK]), ps("pH", [P, 2, BANK])
    pR, pM = ps("pR", [P, 2, BANK]), ps("pM", [P, BANK])
    y_here = [m.sem(f"{name}p_y_here{p}") for p in range(2)]
    x_stored = [m.sem(f"{name}p_x_stored{p}") for p in range(2)]
    h_stored = [m.sem(f"{name}p_h_stored{p}") for p in range(2)]
    loaded, var_ready, std_ready, moments_ready, x_ready, transposed, xT_ready, projected, h_ready, f_done, summed, sum_start, \
        tops, maxed, args, exps, rowsT, rows_out, rows_stored, meaned, chain = (m.sem(f"{name}p_{n}") for n in (
            "loaded", "var_ready", "std_ready", "moments_ready", "x_ready", "transposed", "xT_ready", "projected", "h_ready", "f_done",
            "summed", "sum_start", "tops", "maxed", "args", "exps", "rowsT", "rows_out", "rows_stored", "meaned",
            "chain"))
    n_loads = C + 2 + (2 if b1 is not None else 0)
    with nc.Block() as block:
        @block.sync
        def _(sp):
            for c in range(C):
                sp.dma_start(W[:, c].rearrange("p (h o) -> p h o", h=H) if H > 1 else W[:, c],
                             layer["W"][c * P:(c + 1) * P]).then_inc(loaded, 16)
            sp.dma_start(a1[:], layer["a1"].partition_broadcast(P)).then_inc(loaded, 16)
            sp.dma_start(a2[:], layer["a2"].partition_broadcast(P)).then_inc(loaded, 16)
            if b1 is not None:
                sp.dma_start(b1_wide[:], b1.partition_broadcast(P)).then_inc(loaded, 16)
                sp.dma_start(b2_wide[:], b2.partition_broadcast(P)).then_inc(loaded, 16)

            def load(t, p, left):
                sp.wait_ge(x_ready, t + 1)
                sp.dma_start(y_in[:, p], row_tile(m.y, t)).then_inc(y_here[p], 16)

            each_tile(sp, load)
            for q in range(PARTS):
                sp.wait_ge(rows_out, q + 1)
                heads = m.rows[q * (H // PARTS):(q + 1) * (H // PARTS)]
                sp.dma_start(heads.rearrange("h (t p) -> (h t) p", p=P), rT[0:ROWS, q]).then_inc(rows_stored, 16)
            sp.wait_ge(rows_stored, 16 * PARTS)

        @block.gpsimd
        def _(pool):
            own = Chain(pool, summed)
            nc.gpsimd.memset(h_sum[:], 0.0).then_inc(sum_start, 1)
            pool.wait_ge(sum_start, 1)

            def step(t, p, left):
                pool.wait_ge(h_ready, t + 3)
                own.at(t + 2)
                rows = P if left else LAST
                own.link(nc.gpsimd.tensor_tensor(h_sum[0:rows], h_sum[0:rows], h_out[0:rows, p], ALU.add))

            each_tile(pool, step)
            pool.wait_ge(tops, 1)
            nc.gpsimd.partition_all_reduce(f2_max[:], f2_top[:], P, RMAX).then_inc(maxed, 1)

        @block.tensor
        def _(pe):
            def transposes(t, p):
                pe.wait_ge(x_ready, t + 3)
                pe.wait_ge(xT_ready, t + 1)
                for c in range(C):
                    last = nc.tensor.transpose(pT[:, p, c * P:(c + 1) * P], x_out[:, p, c * P:(c + 1) * P], m.ident[:])
                last.then_inc(transposed, 1)

            def step(t, p, left):
                pe.wait_ge(xT_ready, t + 3)
                pe.wait_ge(h_ready, t + 1)
                for c in range(C):
                    last = nc.tensor.matmul(pH[:, p], xT[:, p, c], W[:, c], start=c == 0, stop=c == C - 1)
                last.then_inc(projected, 1)
                if left >= 2:
                    transposes(t + 2, p)

            pe.wait_ge(loaded, 16 * n_loads)
            transposes(0, 0)
            transposes(1, 1)
            each_tile(pe, step)
            pe.wait_ge(summed, T + 2)
            nc.tensor.matmul(pM[:], over_n[:], h_sum[:], start=True, stop=True).then_inc(meaned, 1)
            pe.wait_ge(exps, 3)
            flat = R[:].rearrange("p h t -> p (h t)")
            for q in range(PARTS):
                nc.tensor.transpose(pR[0:ROWS, q, 0:P], flat[:, q * ROWS:(q + 1) * ROWS], m.ident[:]).then_inc(rowsT, 1)

        @block.scalar
        def _(act):
            act.sem_inc(xT_ready, 2)
            act.wait_ge(var_ready, 1)
            nc.scalar.activation(work[:], work[:], ACT.Sqrt).then_inc(std_ready, 1)

            def normalise(t, p):
                act.wait_ge(y_here[p], (t - p) * 8 + 16)
                act.wait_ge(transposed, t + 1)
                act.wait_ge(x_stored[p], (t - p) * 8 + 16)
                nc.scalar.activation(x_out[:, p], y_in[:, p], ACT.Identity, scale=rstd[:, bass.ts(t, 1)],
                                     bias=shift[:, bass.ts(t, 1)]).then_inc(x_ready, 1)
                act.wait_ge(x_ready, t + 3)
                act.dma_start(row_tile(m.x, t), x_out[:, p]).then_inc(x_stored[p], 16)

            def copy_xT(t, p):
                act.wait_ge(transposed, t + 3)
                act.wait_ge(projected, t + 1)
                nc.scalar.activation(xT[:, p].rearrange("p c i -> p (c i)"), pT[:, p], ACT.Copy).then_inc(xT_ready, 1)

            def step(t, p, left):
                if left >= 2:
                    normalise(t + 2, p)
                if b1 is None:
                    act.wait_ge(projected, t + 3)
                    act.wait_ge(f_done, t * 2 + 2)
                    act.wait_ge(summed, t + 1)
                    act.wait_ge(h_stored[p], (t - p) * 8 + 16)
                    nc.scalar.activation(h_out[:, p], pH[:, p], ACT.Copy).then_inc(h_ready, 1)
                if left >= 2:
                    copy_xT(t + 2, p)
                act.wait_ge(h_ready, t + 3)
                act.dma_start(row_tile(m.h, t), h_out[:, p]).then_inc(h_stored[p], 16)

            act.wait_ge(moments_ready, 1)
            for t in range(2):
                normalise(t, t)
            for t in range(2):
                copy_xT(t, t)
            each_tile(act, step)
            for p in range(2):
                act.wait_ge(x_stored[p], 16 * (T // 2 + 1))
                act.wait_ge(h_stored[p], 16 * (T // 2 + 1))
            for n, t in enumerate((m.b, m.u, R)):
                act.wait_ge(args, n + 1)
                nc.scalar.activation(t[:, 0:H], t[:, 0:H], ACT.Exp).then_inc(exps, 1)

        @block.vector
        def _(dve):
            v = nc.vector
            own = Chain(dve, chain)
            own.link(v.memset(over_n[:], 1.0 / N))
            dve.sem_inc(x_ready, 2)
            dve.sem_inc(projected, 2)
            dve.sem_inc(transposed, 2)
            dve.sem_inc(h_ready, 2)
            dve.sem_inc(f_done, 4)
            dve.sem_inc(summed, 2)
            for p in range(2):
                dve.sem_inc(x_stored[p], 16)
                dve.sem_inc(h_stored[p], 16)

            def std(w):
                dve.sem_inc(var_ready, 1)

            load_moments(nc, dve, own, m, mean, rstd, work, std)
            dve.wait_ge(std_ready, 1)
            own.link(v.reciprocal(rstd[:], work[:]))
            v.scalar_tensor_tensor(out=shift[:], in0=mean[:], scalar=-1.0, in1=rstd[:], op0=ALU.mult,
                                   op1=ALU.mult).then_inc(moments_ready, 1)
            dve.wait_ge(loaded, 16 * n_loads)
            before = MOMENT_LINKS + 2

            def step(t, p, left):
                if b1 is not None:
                    dve.wait_ge(projected, t + 3)
                    dve.wait_ge(summed, t + 1)
                    dve.wait_ge(h_stored[p], (t - p) * 8 + 16)
                    v.tensor_tensor(h_out[:, p], pH[:, p], b1_wide[:], ALU.add).then_inc(h_ready, 1)
                dve.wait_ge(h_ready, t + 3)
                own.at(t * 2 + before)
                flat = lambda a: a[:].rearrange("p h o -> p (h o)")
                dve.wait_ge(f_done, t * 2 + 4)
                own.link(v.tensor_tensor(prod[:, 0], h_out[:, p], flat(a1), ALU.mult))
                own.link(v.tensor_tensor(prod[:, 1], h_out[:, p], flat(a2), ALU.mult))
                for n, f in enumerate((f1, f2)):
                    v.tensor_reduce(f[:, :, t], prod[:, n].rearrange("p (h o) -> p h o", h=H), AX,
                                    ALU.add).then_inc(f_done, 1)

            each_tile(dve, step)
            own.at(T * 2 + before)
            dve.wait_ge(f_done, 2 * T + 4)
            v.tensor_reduce(f2_top[:], f2[:], AX, ALU.max).then_inc(tops, 1)
            dve.wait_ge(maxed, 1)
            wide = lambda a: a[:].rearrange("p (h o) -> p h o", o=1).broadcast_to([P, H, T])
            own.link(v.tensor_tensor(f2[:], f2[:], wide(f2_max), ALU.subtract))
            v.tensor_scalar(m.b[:, 0:H], f2[:], B_SHIFT, None, ALU.add).then_inc(args, 1)
            v.tensor_scalar(m.u[:, 0:H], f2[:], -(1 - SLOPE), -U_SHIFT, ALU.mult, ALU.add).then_inc(args, 1)
            own.link(v.tensor_tensor(f1[:], f1[:], wide(f2_max), ALU.add))
            if b2 is not None:
                own.link(v.tensor_scalar(f1[:], f1[:], b2_wide[:], None, ALU.add))
            own.link(v.tensor_scalar(f1[:], f1[:], 1 - SLOPE, -U_SHIFT, ALU.mult, ALU.add))
            v.tensor_scalar(R[:], f1[:], R_TOP, None, ALU.min).then_inc(args, 1)
            dve.wait_ge(meaned, 1)
            v.tensor_copy(m.mean_h[:], pM[:])
            for q in range(PARTS):
                dve.wait_ge(rowsT, q + 1)
                v.tensor_copy(rT[0:ROWS, q], pR[0:ROWS, q, 0:P]).then_inc(rows_out, 1)


class Finish:

    def __init__(self, nc, sb, m, name, elu):
        self.nc, self.m, self.elu = nc, m, elu
        self.rden = sb("rden", [P, 8])
        self.share = sb("share", [P, 2, D])
        self.neg = sb("neg", [P, 2, D])
        self.x_in = sb("x_in", [P, 2, D])
        self.y = sb("y_out", [P, 2, D])
        self.x_here = [m.sem(f"{name}_x_here{p}") for p in range(2)]
        self.y_stored = [m.sem(f"{name}_y_stored{p}") for p in range(2)]
        self.shared, self.negated, self.exped, self.y_ready, self.acc_read, self.chain, self.chain2 = (
            m.sem(f"{name}_{n}") for n in ("shared", "negated", "exped", "y_ready", "acc_read", "chain", "chain2"))

    def start(self, dve):
        dve.sem_inc(self.y_ready, 2)
        for p in range(2):
            dve.sem_inc(self.y_stored[p], 16)
        self.own, self.own2 = Chain(dve, self.chain), Chain(dve, self.chain2)
        dve.sem_inc(self.acc_read, 2)

    def load_x(self, eng, t, p):
        eng.wait_ge(self.y_ready, t + 1)
        eng.dma_start(self.x_in[:, p], row_tile(self.m.x, t)).then_inc(self.x_here[p], 16)

    def store_y(self, eng, t, p):
        eng.wait_ge(self.y_ready, t + 3)
        eng.dma_start(row_tile(self.m.y, t), self.y[:, p]).then_inc(self.y_stored[p], 16)

    def all_stored(self, eng):
        for p in range(2):
            eng.wait_ge(self.y_stored[p], 16 * (T // 2 + 1))

    def exp_neg(self, act, t, p):
        act.wait_ge(self.shared, t + 1)
        act.wait_ge(self.y_ready, t + 1)
        self.nc.scalar.activation(self.neg[:, p], self.share[:, p], ACT.Relu, scale=-1.0).then_inc(self.negated, 1)
        act.wait_ge(self.negated, t + 1)
        self.nc.scalar.activation(self.neg[:, p], self.neg[:, p], ACT.Exp, scale=-1.0).then_inc(self.exped, 1)

    def divide(self, dve, t, p, den, pieces):
        v, m, own, share = self.nc.vector, self.m, self.own, self.share[:, p]
        own.at(t * 2)
        heads = den.shape[1]
        own.link(v.tensor_scalar(self.rden[:, 0:heads], den, m.empty[:, bass.ts(t, 1)], None, ALU.add))
        own.link(v.reciprocal(self.rden[:, 0:heads], self.rden[:, 0:heads]))
        if heads == 1:
            for to, num in pieces:
                last = v.tensor_scalar(share[:, to], num, self.rden[:, 0:1], None, ALU.mult)
        else:
            r = self.rden[:, 0:heads].rearrange("p (h o) -> p h o", o=1).broadcast_to([P, heads, D // heads])
            last = v.tensor_tensor(share.rearrange("p (h o) -> p h o", h=heads),
                                   pieces.rearrange("p (h o) -> p h o", h=heads), r, ALU.mult)
        last.then_inc(self.acc_read, 1)
        dve.wait_ge(self.acc_read, t + 3)
        v.scalar_tensor_tensor(out=share, in0=m.mean_h[:], scalar=m.empty[:, bass.ts(t, 1)], in1=share,
                               op0=ALU.mult, op1=ALU.add).then_inc(self.shared, 1)

    def residual(self, dve, t, p):
        v, m, own, share, neg = self.nc.vector, self.m, self.own2, self.share[:, p], self.neg[:, p]
        own.at(t * 2 if self.elu else t)
        dve.wait_ge(self.x_here[p], (t - p) * 8 + 16)
        dve.wait_ge(self.y_stored[p], (t - p) * 8 + 16)
        dve.wait_ge(self.shared, t + 1)
        if self.elu:
            dve.wait_ge(self.exped, t + 1)
            own.link(v.scalar_tensor_tensor(out=neg, in0=share, scalar=0.0, in1=neg, op0=ALU.max, op1=ALU.add))
            ins = v.scalar_tensor_tensor(out=self.y[:, p], in0=neg, scalar=-1.0, in1=self.x_in[:, p],
                                         op0=ALU.add, op1=ALU.add)
        else:
            ins = v.tensor_tensor(self.y[:, p], share, self.x_in[:, p], ALU.add)
        ins.then_inc(self.y_ready, 1)
        dve.wait_ge(self.y_ready, t + 3)
        own.link(v.bn_stats(m.stats[:, t], self.y[:, p]))


def attend_one_head(nc, ctx, m, name):
    sb = lambda n, s, d=F32: ctx.enter_context(nc.sbuf_tensor(f"{name}a_{n}", s, d))
    W = 2 * P
    CH = T // 2
    RING = 4
    LEFT = D // 2
    R = sb("R", [P, NP])
    V = sb("V", [P, T, D + 1])
    weights = sb("weights", [P, RING, W])
    acc = ctx.enter_context(nc.psum_tensor(f"{name}a_acc", [P, 2, 2, 2, BANK], F32))
    fin = Finish(nc, sb, m, name + "a", True)
    r_here, v_here, b_in, v_ready, w_ready, w_used, chunk_done = (m.sem(f"{name}a_{n}") for n in (
        "r_here", "v_here", "b_in", "v_ready", "w_ready", "w_used", "chunk_done"))

    def each_chunk(eng, first, body):
        first()
        with eng.Fori(0, (CH - 1) // 2) as pair:
            for q in range(2):
                body(pair * 2 + 1 + q, (1 + q) % 2, (1 + q) * T % RING)

    with nc.Block() as block:
        @block.sync
        def _(sp):
            sp.dma_start(R[:], m.rows[0].partition_broadcast(P)).then_inc(r_here, 16)
            h = m.h.rearrange("(t p) d -> p t d", p=P)
            for j in range(T):
                sp.dma_start(V[:, j, 0:D], h[:, j]).then_inc(v_here, 16)
            each_tile(sp, lambda t, p, left: fin.load_x(sp, t, p))

        @block.scalar
        def _(act):
            def fin_step(t, p, left):
                fin.exp_neg(act, t, p)
                fin.store_y(act, t, p)

            act.wait_ge(v_here, 16 * T)
            for j in range(T):
                nc.scalar.activation(V[:, j, 0:D], V[:, j, 0:D], ACT.Copy, scale=m.b[:, 0, j:j + 1]).then_inc(v_ready, 1)
            each_tile(act, fin_step)
            fin.all_stored(act)

        @block.tensor
        def _(pe):
            def chunk(c, cp, ring, first):
                for j in range(T):
                    if first:
                        pe.wait_ge(v_ready, j + 1)
                    if j == 0:
                        pe.wait_ge(fin.acc_read, c * 2)
                    pe.wait_ge(w_ready, c * T + j + 1)
                    for i in range(2):
                        w = weights[:, (ring + j) % RING, i * P:(i + 1) * P]
                        nc.tensor.matmul(acc[:, cp, i, 0, 0:D + 1 - LEFT], w, V[:, j, LEFT:D + 1],
                                         start=j == 0, stop=j == T - 1)
                        last = nc.tensor.matmul(acc[:, cp, i, 1, 0:LEFT], w, V[:, j, 0:LEFT],
                                                start=j == 0, stop=j == T - 1)
                    last.then_inc(w_used, 1)

            pe.sem_inc(w_used, RING)
            pe.wait_ge(b_in, 1)
            each_chunk(pe, lambda: chunk(0, 0, 0, True), lambda c, cp, ring: chunk(c, cp, ring, False))

        @block.vector
        def _(dve):
            v = nc.vector
            fin.start(dve)
            v.tensor_copy(V[:, :, D:D + 1].rearrange("p t o -> p (t o)"), m.b[:, 0]).then_inc(b_in, 1)
            dve.wait_ge(r_here, 16)

            def make(c, j, ring):
                dve.wait_ge(w_used, c * T + j + 1)
                v.scalar_tensor_tensor(out=weights[:, (ring + j) % RING], in0=R[:, bass.ts(c, W)],
                                       scalar=m.u[:, 0, j:j + 1], in1=m.mask[:, j, bass.ts(c, W)],
                                       op0=ALU.max, op1=ALU.mult).then_inc(w_ready, 1)

            def divide(c, cp, i):
                dve.wait_ge(w_used, (c + 1) * T + RING)
                a = acc[:, cp, i]
                fin.divide(dve, c * 2 + i, i, a[:, 0, D - LEFT:D - LEFT + 1],
                           [(slice(0, LEFT), a[:, 1, 0:LEFT]), (slice(LEFT, D), a[:, 0, 0:D - LEFT])])

            def first():
                for j in range(T):
                    make(0, j, 0)

            def chunk(c, cp, ring):
                for j in range(T):
                    make(c, j, ring)
                    if j in (4, 14):
                        divide(c - 1, 1 - cp, (j - 4) // 10)
                    if j in (8, 18):
                        i = (j - 8) // 10
                        fin.residual(dve, (c - 1) * 2 + i, i)

            each_chunk(dve, first, chunk)
            for i in range(2):
                divide(CH - 1, (CH - 1) % 2, i)
                fin.residual(dve, (CH - 1) * 2 + i, i)


def attend_heads(nc, ctx, m, name, H):
    O = D // H
    PER, PICK = 5, (1, 3)
    GROUPS = T // PER
    split = [PER * g + q for g in range(GROUPS) for q in PICK]
    HALF, BANKS, RING = NP // 2, 4, 4
    WIDTH = HALF // BANKS
    UNITS = 2 * H
    sb = lambda n, s, d=F32: ctx.enter_context(nc.sbuf_tensor(f"{name}a_{n}", s, d))
    R = sb("R", [P, 2, HALF])
    V = sb("V", [P, 2, T, O + 1])
    V_high = sb("V_high", [P, 2, len(split), O + 1], F32R)
    V_low = sb("V_low", [P, 2, len(split), O + 1], F32R)
    weights = sb("weights", [P, RING, HALF])
    w_high = sb("w_high", [P, 2, HALF], F32R)
    w_low = sb("w_low", [P, 2, HALF], F32R)
    sums = sb("sums", [P, HALF])
    acc = ctx.enter_context(nc.psum_tensor(f"{name}a_acc", [P, 2, BANKS, BANK], F32))
    r_here = [m.sem(f"{name}a_r_here{p}") for p in range(2)]
    v_here = [m.sem(f"{name}a_v_here{p}") for p in range(2)]
    v_scaled, v_cut, v_ready, w_ready, w_used, high_ready, low_ready, evacuated, stored = (
        m.sem(f"{name}a_{n}") for n in ("v_scaled", "v_cut", "v_ready", "w_ready", "w_used", "high_ready", "low_ready",
                                        "evacuated", "stored"))

    def each_unit(eng, body):
        with eng.Fori(0, 2) as half:
            with eng.Fori(0, H // 2) as pair:
                for p in range(2):
                    h = pair * 2 + p
                    body(half * H + h, half, h, p)

    nums = m.num.rearrange("(s t) h o n -> s h o t n", s=2)
    dens = m.den.rearrange("(s t) (h a) n -> s h a t n", s=2, a=1)

    def cut_parts(p, q):
        high, low = (a[:, p].rearrange("p (g f) o -> p g f o", f=len(PICK))[:, :, q] for a in (V_high, V_low))
        return V[:, p, 0:PER * GROUPS].rearrange("p (g f) o -> p g f o", f=PER)[:, :, PICK[q]], high, low

    with nc.Block() as block:
        @block.sync
        def _(sp):
            values = m.h.rearrange("(t p) (h o) -> h p t o", p=P, h=H)

            def load(n, half, h, p):
                sp.wait_ge(w_ready, (n + 1) * T)
                sp.dma_start(R[:, p], m.rows[h][bass.ts(half, HALF)].partition_broadcast(P)).then_inc(r_here[p], 16)
                sp.wait_ge(w_used, (n + 1) * T)
                sp.dma_start(V[:, p, :, 0:O], values[h]).then_inc(v_here[p], 16)

            each_unit(sp, load)

        @block.gpsimd
        def _(pool):
            def values(n, half, h, p):
                pool.wait_ge(v_here[p], (n - p) * 8 + 16)
                b = m.b[:, h].rearrange("p (t o) -> p t o", o=1)
                nc.gpsimd.tensor_tensor(V[:, p, :, 0:O], V[:, p, :, 0:O], b.broadcast_to([P, T, O]),
                                        ALU.mult).then_inc(v_scaled, 1)
                nc.gpsimd.tensor_copy(V[:, p, :, O:O + 1], b).then_inc(v_scaled, 1)
                for q in range(len(PICK)):
                    whole, high, low = cut_parts(p, q)
                    pool.wait_ge(v_cut, n * len(PICK) + q + 1)
                    nc.gpsimd.tensor_tensor(low, whole, high.bitcast(F32), ALU.subtract).then_inc(v_ready, 1)

            each_unit(pool, values)

        @block.vector
        def _(dve):
            dve.sem_inc(w_ready, 2 * T)

            def unit(n, half, h, p):
                def cut(j):
                    s = split.index(j)
                    dve.wait_ge(high_ready, n * len(split) + s + 1)
                    nc.vector.tensor_tensor(w_low[:, s % 2], weights[:, (p * T + j) % RING],
                                            w_high[:, s % 2].bitcast(F32), ALU.subtract).then_inc(low_ready, 1)

                dve.wait_ge(r_here[p], (n - p) * 8 + 16)
                for j in range(T):
                    dve.wait_ge(w_used, (n + 2) * T + j + 1 - RING)
                    nc.vector.scalar_tensor_tensor(out=weights[:, (p * T + j) % RING], in0=R[:, p],
                                                   scalar=m.u[:, h, j:j + 1], in1=m.mask[:, j, bass.ts(half, HALF)],
                                                   op0=ALU.max, op1=ALU.mult).then_inc(w_ready, 1)
                    if j - 1 in split:
                        cut(j - 1)

            each_unit(dve, unit)

        @block.tensor
        def _(pe):
            pe.sem_inc(w_used, 2 * T)

            def unit(n, half, h, p):
                pe.wait_ge(v_ready, (n + 1) * len(PICK))
                pe.wait_ge(evacuated, (n + 1) * BANKS)
                for j in range(T):
                    if j in split:
                        s = split.index(j)
                        pe.wait_ge(low_ready, n * len(split) + s + 1)
                        products = [(V_high[:, p, s], w_high[:, s % 2]), (V_low[:, p, s], w_high[:, s % 2]),
                                    (V_high[:, p, s], w_low[:, s % 2])]
                    else:
                        pe.wait_ge(w_ready, (n + 2) * T + j + 1)
                        products = [(V[:, p, j], weights[:, (p * T + j) % RING])]
                    for v, w in products:
                        for k in range(BANKS):
                            last = nc.tensor.matmul(acc[0:O + 1, p, k, 0:WIDTH], v, w[:, k * WIDTH:(k + 1) * WIDTH],
                                                    start=j == 0, stop=j == T - 1)
                    last.then_inc(w_used, 1)

            each_unit(pe, unit)

        @block.scalar
        def _(act):
            act.sem_inc(evacuated, 2 * BANKS)
            act.sem_inc(stored, 32)

            def evacuate(n, p):
                act.wait_ge(stored, n * 32 + 32)
                act.wait_ge(w_used, (n + 3) * T)
                for k in range(BANKS):
                    nc.scalar.activation(sums[0:O + 1, k * WIDTH:(k + 1) * WIDTH], acc[0:O + 1, p, k, 0:WIDTH],
                                         ACT.Copy).then_inc(evacuated, 1)
                act.wait_ge(evacuated, (n + 3) * BANKS)
                half, h = n // H, n % H
                tiles = sums[:].rearrange("o (t n) -> o t n", n=P)
                act.dma_start(nums[half][h], tiles[0:O]).then_inc(stored, 16)
                act.dma_start(dens[half][h], tiles[O:O + 1]).then_inc(stored, 16)

            def cut_values(n, p):
                act.wait_ge(v_scaled, (n + 1) * 2)
                act.wait_ge(w_used, (n + 1) * T)
                for q in range(len(PICK)):
                    whole, high, _ = cut_parts(p, q)
                    nc.scalar.activation(high, whole, ACT.Copy).then_inc(v_cut, 1)

            def unit(n, p, is_first=False, left=1):
                for s, j in enumerate(split):
                    if s == 2 and not is_first:
                        evacuate(n - 1, 1 - p)
                    if s == 5 and left:
                        cut_values(n + 1, 1 - p)
                    act.wait_ge(w_ready, (n + 2) * T + j + 1)
                    act.wait_ge(w_used, (n + (2 if s >= 2 else 1)) * T + split[s - 2] + 1)
                    nc.scalar.activation(w_high[:, s % 2], weights[:, (p * T + j) % RING], ACT.Copy).then_inc(high_ready, 1)

            cut_values(0, 0)
            unit(0, 0, is_first=True)
            with act.Fori(0, UNITS // 2 - 1) as pair:
                for q in range(2):
                    unit(pair * 2 + 1 + q, (1 + q) % 2)
            unit(UNITS - 1, 1, left=0)
            evacuate(UNITS - 1, 1)
            act.wait_ge(stored, UNITS * 32 + 32)


def finish_heads(nc, ctx, m, name, H, elu, out):
    O = D // H
    sb = lambda n, s, d=F32: ctx.enter_context(nc.sbuf_tensor(f"{name}f_{n}", s, d))
    num = sb("num", [P, 2, C, P])
    den = sb("den", [H, 2, P])
    mean, spread, squares = (sb(n, [P, 2]) for n in ("mean", "spread", "squares"))
    std = sb("std", [P, 2])
    rstd = sb("rstd", [P, 2])
    x_out = sb("x_out", [P, 2, D])
    pN = ctx.enter_context(nc.psum_tensor(f"{name}f_pN", [P, 2, BANK], F32))
    pD = ctx.enter_context(nc.psum_tensor(f"{name}f_pD", [P, 2, BANK], F32))
    fin = Finish(nc, sb, m, name + "f", elu)
    here = [m.sem(f"{name}f_here{p}") for p in range(2)]
    out_stored = [m.sem(f"{name}f_out_stored{p}") for p in range(2)]
    turned, halves, var_ready, std_ready, normal, chain3 = (m.sem(f"{name}f_{n}") for n in (
        "turned", "halves", "var_ready", "std_ready", "normal", "chain3"))
    with nc.Block() as block:
        @block.sync
        def _(sp):
            pairs = m.num.rearrange("t (c a) o n -> t (a o) c n", a=P // O)

            def load(t, p, left):
                sp.wait_ge(turned, t + 1)
                sp.dma_start(num[:, p], pairs[t]).then_inc(here[p], 16)
                sp.dma_start(den[:, p], m.den[t]).then_inc(here[p], 16)
                fin.load_x(sp, t, p)

            each_tile(sp, load)

        @block.tensor
        def _(pe):
            pe.sem_inc(turned, 2)

            def turn(t, p, left):
                pe.wait_ge(here[p], (t - p) * 16 + 32)
                pe.wait_ge(fin.acc_read, t + 1)
                for c in range(C):
                    nc.tensor.transpose(pN[:, p, c * P:(c + 1) * P], num[:, p, c], m.ident[:])
                nc.tensor.transpose(pD[:, p, 0:H], den[:, p], m.ident[0:H, 0:H]).then_inc(turned, 1)

            each_tile(pe, turn)

        @block.scalar
        def _(act):
            def step(t, p, left):
                if elu:
                    fin.exp_neg(act, t, p)
                if out is None:
                    fin.store_y(act, t, p)
                    return
                act.wait_ge(var_ready, t + 1)
                nc.scalar.activation(std[:, p:p + 1], std[:, p:p + 1], ACT.Sqrt).then_inc(std_ready, 1)
                act.wait_ge(normal, t + 1)
                if left:
                    act.dma_start(out[0:(T - 1) * P].rearrange("(t p) d -> t p d", p=P)[t],
                                  x_out[:, p]).then_inc(out_stored[p], 16)
                else:
                    act.dma_start(out[(T - 1) * P:N], x_out[0:LAST, p]).then_inc(out_stored[p], 16)

            each_tile(act, step)
            if out is None:
                fin.all_stored(act)
            else:
                for p in range(2):
                    act.wait_ge(out_stored[p], 16 * (T // 2 + 1))

        @block.vector
        def _(dve):
            v = nc.vector
            own = Chain(dve, chain3)
            fin.start(dve)
            for p in range(2):
                dve.sem_inc(out_stored[p], 16)
            if out is not None:
                for p in range(2):
                    dve.sem_inc(fin.y_stored[p], 16 * T)

            def divide(t, p):
                dve.wait_ge(turned, t + 3)
                fin.divide(dve, t, p, pD[:, p, 0:H], pN[:, p])

            def variance(t, p):
                st, one = m.stats[:, t], slice(p, p + 1)
                v.tensor_tensor(mean[:, one], st[:, 1:2], st[:, 4:5], ALU.add).then_inc(halves, 1)
                v.tensor_tensor(spread[:, one], st[:, 1:2], st[:, 4:5], ALU.subtract).then_inc(halves, 1)
                v.tensor_tensor(squares[:, one], st[:, 2:3], st[:, 5:6], ALU.add).then_inc(halves, 1)
                dve.wait_ge(halves, t * 6 + 3)
                v.tensor_scalar(mean[:, one], mean[:, one], 0.5, None, ALU.mult).then_inc(halves, 1)
                v.scalar_tensor_tensor(out=spread[:, one], in0=spread[:, one], scalar=0.25, in1=spread[:, one],
                                       op0=ALU.mult, op1=ALU.mult).then_inc(halves, 1)
                v.tensor_scalar(squares[:, one], squares[:, one], 1.0 / D, EPS, ALU.mult, ALU.add).then_inc(halves, 1)
                dve.wait_ge(halves, t * 6 + 6)
                v.tensor_tensor(std[:, one], squares[:, one], spread[:, one], ALU.add).then_inc(var_ready, 1)

            def normalise(t, p):
                own.at(t)
                dve.wait_ge(std_ready, t + 1)
                own.link(v.reciprocal(rstd[:, p:p + 1], std[:, p:p + 1]))
                dve.wait_ge(out_stored[p], (t - p) * 8 + 16)
                v.tensor_scalar(x_out[:, p], fin.y[:, p], mean[:, p:p + 1], rstd[:, p:p + 1], ALU.subtract,
                                ALU.mult).then_inc(normal, 1)

            def step(t, p, left):
                if out is None:
                    if left:
                        divide(t + 1, 1 - p)
                    fin.residual(dve, t, p)
                else:
                    fin.residual(dve, t, p)
                    variance(t, p)
                    if left:
                        divide(t + 1, 1 - p)
                    normalise(t, p)

            divide(0, 0)
            each_tile(dve, step)


_INS = ["x", "adj", "L0_gnn_W_self", "L0_gnn_b_self", "L0_gnn_W_nb", "L0_gnn_b_nb", "L0_gnn_W_comb", "L0_gnn_b_comb",
        "L1_gnn_W1", "L1_gnn_b1", "L1_gnn_a1", "L1_gnn_a2", "L1_gnn_b2", "L2_gnn_W", "L2_gnn_a1", "L2_gnn_a2",
        "L3_gnn_W", "L3_gnn_a"]


def kernel(**inputs):
    import numpy as _np
    import concourse.bacc as _bacc
    from concourse import mybir as _mybir
    from concourse.bass_utils import run_bass_kernel_spmd as _run

    nc = _bacc.Bacc("TRN2", target_bir_lowering=False, num_devices=1)
    arrays, args = {}, []
    for name in _INS:
        a = _np.ascontiguousarray(inputs[name]).reshape(_np.shape(inputs[name]) or (1,))
        arrays[f"in_{name}"] = a
        args.append(nc.dram_tensor(f"in_{name}", a.shape, _mybir.dt.from_np(a.dtype), kind="ExternalInput").ap())
    out = nc.dram_tensor("out", (N, D), F32, kind="ExternalOutput").ap()
    gnn_kernel(nc, *args, out)
    r = _run(nc, [arrays], core_ids=[0])
    return r.results[0]["out"]
```

```python
from contextlib import ExitStack

import concourse.bass as bass
from concourse import mybir

ALU = mybir.AluOpType
ACT = mybir.ActivationFunctionType
AX = mybir.AxisListType.X
F32 = mybir.dt.float32
BF16 = mybir.dt.bfloat16
F32R = mybir.dt.float32r
I32 = mybir.dt.int32
U8 = mybir.dt.uint8
RMAX = bass.bass_isa.ReduceOp.max

P = 128
BANK = 512
N = 3327
T = -(-N // P)
NP = T * P
LAST = N - (T - 1) * P
D = 512
C = D // P
SLOPE = 0.2
EPS = 1e-5
B_SHIFT = 30.0
U_SHIFT = 60.0
R_TOP = 45.0


class Chain:

    def __init__(self, eng, sem):
        self.eng, self.sem, self.base, self.n = eng, sem, 0, 0

    def at(self, base):
        self.base, self.n = base, 0

    def link(self, ins):
        ins.then_inc(self.sem, 1)
        self.n += 1
        self.eng.wait_ge(self.sem, self.base + self.n)


def each_tile(eng, step):
    with eng.Fori(0, T // 2 - 1) as pair:
        for p in range(2):
            step(pair * 2 + p, p, 2)
    for p in range(2):
        step(T - 2 + p, p, 1 - p)


def row_tile(dram, t):
    return dram.rearrange("(t p) d -> t p d", p=P)[t]


def gnn_kernel(nc, x, adj, L0_gnn_W_self, L0_gnn_b_self, L0_gnn_W_nb, L0_gnn_b_nb, L0_gnn_W_comb, L0_gnn_b_comb,
               L1_gnn_W1, L1_gnn_b1, L1_gnn_a1, L1_gnn_a2, L1_gnn_b2, L2_gnn_W, L2_gnn_a1, L2_gnn_a2,
               L3_gnn_W, L3_gnn_a, out):
    with ExitStack() as ctx:
        m = Memory(nc, ctx)
        with ExitStack() as first:
            m.zs = first.enter_context(nc.sbuf_tensor("zs", [P, T, 2, D], F32R, side="right"))
            with ExitStack() as s:
                fold_weights(nc, s, m, L0_gnn_W_self, L0_gnn_b_self, L0_gnn_W_nb, L0_gnn_b_nb,
                             L0_gnn_W_comb, L0_gnn_b_comb)
                m.end_stage()
                project_input(nc, s, m, x)
            m.end_stage()
            m.mask = ctx.enter_context(nc.sbuf_tensor("mask", [P, T, NP], U8))
            with ExitStack() as s:
                aggregate(nc, s, m, x, adj)
            m.end_stage()
        head = lambda w: w.rearrange("h d o -> d h o")
        layers = [
            dict(H=1, W=L1_gnn_W1, a1=L1_gnn_a1.rearrange("(h o) -> h o", h=1),
                 a2=L1_gnn_a2.rearrange("(h o) -> h o", h=1), b1=L1_gnn_b1, b2=L1_gnn_b2, elu=True),
            dict(H=8, W=head(L2_gnn_W), a1=L2_gnn_a1, a2=L2_gnn_a2, b1=None, b2=None, elu=True),
            dict(H=8, W=head(L3_gnn_W), a1=L3_gnn_a[:, 0:64], a2=L3_gnn_a[:, 64:128], b1=None, b2=None, elu=False),
        ]
        for n, layer in enumerate(layers, 1):
            with ExitStack() as whole:
                m.attention_state(nc, whole, f"L{n}", layer["H"])
                with ExitStack() as s:
                    project(nc, s, m, f"L{n}", layer)
                m.end_stage()
                with ExitStack() as s:
                    if layer["H"] == 1:
                        attend_one_head(nc, s, m, f"L{n}")
                    else:
                        attend_heads(nc, s, m, f"L{n}", layer["H"])
                m.end_stage()
                if layer["H"] > 1:
                    with ExitStack() as s:
                        finish_heads(nc, s, m, f"L{n}", layer["H"], layer["elu"], out if n == len(layers) else None)
                    m.end_stage()


class Memory:

    def __init__(self, nc, ctx):
        sb = lambda n, s, d: ctx.enter_context(nc.sbuf_tensor(n, s, d))
        dram = lambda n, s: nc.dram_tensor(n, s, F32, kind="Internal").ap()
        self.ident = sb("ident", [P, P], F32)
        self.identb = sb("identb", [P, P], BF16)
        self.empty = sb("empty", [P, T], F32)
        self.stats = sb("stats", [P, T, 6], F32)
        self.y = dram("y_scratch", [NP, D])
        self.x = dram("x_scratch", [NP, D])
        self.self_part = dram("self_scratch", [NP, D])
        self.h = dram("h_scratch", [NP, D])
        self.rows = dram("r_scratch", [8, NP])
        self.num = dram("num_scratch", [T, 8, 64, P])
        self.den = dram("den_scratch", [T, 8, P])
        self.nc, self.stage_sems = nc, []

    def sem(self, name):
        self.stage_sems.append(self.nc.alloc_semaphore(name=name))
        return self.stage_sems[-1]

    def sems(self, prefix, names):
        return [self.sem(prefix + name) for name in names.split()]

    def end_stage(self):
        self.nc.clear_and_free_semaphores(self.stage_sems)
        self.stage_sems = []
        self.nc.all_engine_barrier()

    def attention_state(self, nc, ctx, name, H):
        sb = lambda n, s, d: ctx.enter_context(nc.sbuf_tensor(f"{name}_{n}", s, d))
        self.u = sb("u", [P, H, T], F32)
        self.b = sb("b", [P, H, T], F32)
        self.mean_h = sb("mean_h", [P, D], F32)


def fold_weights(nc, ctx, m, w_self, b_self, w_nb, b_nb, w_comb, b_comb):
    sb = lambda n, s, d=F32: ctx.enter_context(nc.sbuf_tensor(n, s, d))
    m.fold_high, m.fold_low = (sb(n, [P, 2, C, D], F32R) for n in ("fold_high", "fold_low"))
    m.fold_bias = sb("fold_bias", [P, D])
    with ExitStack() as s2:
        sb = lambda n, s, d=F32: s2.enter_context(nc.sbuf_tensor(n, s, d))
        ps = lambda n, s: s2.enter_context(nc.psum_tensor(n, s, F32))
        w_in, wT, wc = (sb(n, [P, 2, C, D]) for n in ("w_in", "wT", "wc"))
        bias_col = sb("bias_col", [P, 2, C])
        bias_wide = sb("bias_wide", [P, 2, C, P])
        bias_comb = sb("bias_comb", [P, D])
        ones = sb("ones_row", [P, P])
        pT = ps("pT", [P, 2, BANK])
        pF = ps("pF", [P, 2, BANK])
        pB = ps("pB", [P, BANK])
        self_here, nb_here, loaded, zeroed, ident_ready, wide, transposed, copied, product, high_done, \
            product_used, bias_done, done = m.sems("fw_",
            "self_here nb_here loaded zeroed ident wide transposed copied product high_done "
            "product_used bias_done done")
        with nc.Block() as block:
            @block.sync
            def _(sp):
                sp.dma_start(w_in[:, 0], w_self.rearrange("(c p) n -> p c n", p=P)).then_inc(self_here, 16)
                sp.dma_start(w_in[:, 1], w_nb.rearrange("(c p) n -> p c n", p=P)).then_inc(nb_here, 16)
                sp.dma_start(wc[:, 0], w_comb[0:D].rearrange("(c p) n -> p c n", p=P)).then_inc(loaded, 16)
                sp.dma_start(wc[:, 1], w_comb[D:2 * D].rearrange("(c p) n -> p c n", p=P)).then_inc(loaded, 16)
                with nc.allow_non_contiguous_dma("two small bias columns"):
                    sp.dma_start(bias_col[:, 0], b_self.rearrange("(c p) -> p c", p=P)).then_inc(loaded, 16)
                    sp.dma_start(bias_col[:, 1], b_nb.rearrange("(c p) -> p c", p=P)).then_inc(loaded, 16)
                sp.dma_start(bias_comb[:], b_comb.partition_broadcast(P)).then_inc(loaded, 16)

            @block.gpsimd
            def _(pool):
                nc.gpsimd.memset(m.ident[:], 0.0).then_inc(zeroed, 1)
                nc.gpsimd.memset(m.identb[:], 0.0).then_inc(zeroed, 1)
                pool.wait_ge(zeroed, 2)
                for t in (m.ident, m.identb):
                    nc.gpsimd.affine_select(out=t[:], in_=t[:], compare_op=ALU.not_equal, fill=1.0, base=0,
                                            pattern=[[-1, P]], channel_multiplier=1).then_inc(ident_ready, 1)

            @block.vector
            def _(dve):
                nc.vector.memset(ones[:], 1.0).then_inc(wide, 1)
                dve.wait_ge(wide, 1)
                dve.wait_ge(loaded, 5 * 16)
                for w in range(2):
                    for c in range(C):
                        nc.vector.tensor_scalar(bias_wide[:, w, c], ones[:], bias_col[:, w, c:c + 1], None,
                                                ALU.mult).then_inc(wide, 1)
                for n in range(2 * C):
                    dve.wait_ge(high_done, n + 1)
                    nc.vector.tensor_tensor(m.fold_low[:, n // C, n % C], pF[:, n % 2],
                                            m.fold_high[:, n // C, n % C].bitcast(F32), ALU.subtract).then_inc(product_used, 1)
                dve.wait_ge(bias_done, 1)
                nc.vector.tensor_tensor(m.fold_bias[:], pB[:], bias_comb[:], ALU.add).then_inc(done, 1)

            @block.scalar
            def _(act):
                for n in range(2 * C):
                    act.wait_ge(transposed, n + 1)
                    nc.scalar.activation(wT[:, n // C, n % C], pT[:, n % 2], ACT.Copy).then_inc(copied, 1)
                for n in range(2 * C):
                    act.wait_ge(product, n + 1)
                    nc.scalar.activation(m.fold_high[:, n // C, n % C], pF[:, n % 2], ACT.Copy).then_inc(high_done, 1)

            @block.tensor
            def _(pe):
                pe.wait_ge(ident_ready, 2)
                for n in range(2 * C):
                    w, c = n // C, n % C
                    if c == 0:
                        pe.wait_ge((self_here, nb_here)[w], 16)
                    if n >= 2:
                        pe.wait_ge(copied, n - 1)
                    for k in range(C):
                        last = nc.tensor.transpose(pT[:, n % 2, k * P:(k + 1) * P],
                                                   w_in[:, w, k, c * P:(c + 1) * P], m.ident[:])
                    last.then_inc(transposed, 1)
                pe.wait_ge(copied, 2 * C)
                pe.wait_ge(loaded, 5 * 16)
                for n in range(2 * C):
                    w, k = n // C, n % C
                    if n >= 2:
                        pe.wait_ge(product_used, n - 1)
                    for c in range(C):
                        last = nc.tensor.matmul(pF[:, n % 2], wT[:, w, c, k * P:(k + 1) * P], wc[:, w, c],
                                                start=c == 0, stop=c == C - 1)
                    last.then_inc(product, 1)
                pe.wait_ge(wide, 2 * C + 1)
                for n in range(2 * C):
                    last = nc.tensor.matmul(pB[:], bias_wide[:, n // C, n % C], wc[:, n // C, n % C],
                                            start=n == 0, stop=n == 2 * C - 1)
                last.then_inc(bias_done, 1)


def product_in_parts(nc, out, xT_high, xT_low, w_high, w_low):
    parts = [(xT_high, w_high), (xT_high, w_low), (xT_low, w_high)]
    for n, (a, w) in enumerate(parts):
        for c in range(C):
            last = nc.tensor.matmul(out, a[:, c], w[:, c], start=n == 0 and c == 0, stop=n == 2 and c == C - 1)
    return last


def project_input(nc, ctx, m, x):
    sb = lambda n, s, d=F32: ctx.enter_context(nc.sbuf_tensor(n, s, d))
    ps = lambda n, s: ctx.enter_context(nc.psum_tensor(n, s, F32))
    x_in = sb("pi_x", [P, 2, D])
    xT_high, xT_low = sb("pi_xT_high", [P, 2, C, P], F32R), sb("pi_xT_low", [P, 2, C, P], F32R)
    self_out = sb("pi_self", [P, 2, D])
    pT, pS, pZ = ps("pi_pT", [P, 2, BANK]), ps("pi_pS", [P, 2, BANK]), ps("pi_pZ", [P, 2, BANK])
    x_here = [m.sem(f"pi_x_here{p}") for p in range(2)]
    stored = [m.sem(f"pi_stored{p}") for p in range(2)]
    cleared, transposed, high_ready, xT_ready, self_ready, self_made, z_ready, z_high, pZ_read = m.sems("pi_",
            "cleared transposed high_ready xT_ready self_ready self_made z_ready z_high pZ_read")
    with nc.Block() as block:
        @block.sync
        def _(sp):
            sp.wait_ge(cleared, 1)

            def load(t, p, left):
                sp.wait_ge(transposed, t + 1)
                if not left:
                    sp.dma_start(x_in[0:LAST, p], x[(T - 1) * P:N]).then_inc(x_here[p], 16)
                else:
                    full = x[0:(T - 1) * P].rearrange("(t p) d -> t p d", p=P)
                    sp.dma_start(x_in[:, p], full[t]).then_inc(x_here[p], 16)

            each_tile(sp, load)

        @block.gpsimd
        def _(pool):
            nc.gpsimd.memset(x_in[:], 0.0).then_inc(cleared, 1)

        @block.tensor
        def _(pe):
            def transposes(t, p):
                pe.wait_ge(x_here[p], (t - p) * 8 + 16)
                pe.wait_ge(xT_ready, t + 1)
                for c in range(C):
                    last = nc.tensor.transpose(pT[:, p, c * P:(c + 1) * P], x_in[:, p, c * P:(c + 1) * P], m.ident[:])
                last.then_inc(transposed, 1)

            def products(t, p, left):
                if left:
                    transposes(t + 1, 1 - p)
                pe.wait_ge(xT_ready, t + 3)
                pe.wait_ge(self_made, t + 1)
                product_in_parts(nc, pS[:, p], xT_high[:, p], xT_low[:, p], m.fold_high[:, 0], m.fold_low[:, 0])\
                    .then_inc(self_ready, 1)
                pe.wait_ge(pZ_read, t + 1)
                product_in_parts(nc, pZ[:, p], xT_high[:, p], xT_low[:, p], m.fold_high[:, 1], m.fold_low[:, 1])\
                    .then_inc(z_ready, 1)

            pe.sem_inc(transposed, 2)
            pe.sem_inc(z_ready, 2)
            transposes(0, 0)
            each_tile(pe, products)

        @block.scalar
        def _(act):
            def copy_xT(t, p):
                act.wait_ge(transposed, t + 3)
                act.wait_ge(z_ready, t + 1)
                nc.scalar.activation(xT_high[:, p].rearrange("p c i -> p (c i)"), pT[:, p], ACT.Copy).then_inc(high_ready, 1)

            def step(t, p, left):
                if left:
                    copy_xT(t + 1, 1 - p)
                act.wait_ge(z_ready, t + 3)
                nc.scalar.activation(m.zs[:, t, 0], pZ[:, p], ACT.Copy).then_inc(z_high, 1)
                act.wait_ge(self_made, t + 3)
                act.dma_start(row_tile(m.self_part, t), self_out[:, p]).then_inc(stored[p], 16)

            copy_xT(0, 0)
            each_tile(act, step)
            for p in range(2):
                act.wait_ge(stored[p], 16 * (T // 2 + 1))

        @block.vector
        def _(dve):
            dve.sem_inc(self_made, 2)
            dve.sem_inc(pZ_read, 2)
            for p in range(2):
                dve.sem_inc(stored[p], 16)
            dve.sem_inc(xT_ready, 2)

            def cut_xT(t, p):
                dve.wait_ge(high_ready, t + 1)
                flat = lambda a: a[:, p].rearrange("p c i -> p (c i)")
                nc.vector.tensor_tensor(flat(xT_low), pT[:, p], flat(xT_high).bitcast(F32),
                                        ALU.subtract).then_inc(xT_ready, 1)

            cut_xT(0, 0)

            def step(t, p, left):
                if left:
                    cut_xT(t + 1, 1 - p)
                dve.wait_ge(self_ready, t + 1)
                dve.wait_ge(stored[p], (t - p) * 8 + 16)
                nc.vector.tensor_tensor(self_out[:, p], pS[:, p], m.fold_bias[:], ALU.add).then_inc(self_made, 1)
                dve.wait_ge(z_high, t + 1)
                nc.vector.tensor_tensor(m.zs[:, t, 1], pZ[:, p], m.zs[:, t, 0].bitcast(F32), ALU.subtract)\
                    .then_inc(pZ_read, 1)

            each_tile(dve, step)


def aggregate(nc, ctx, m, x, adj):
    sb = lambda n, s, d=F32: ctx.enter_context(nc.sbuf_tensor(n, s, d))
    CHUNK = 3
    CHUNKS = -(-T // CHUNK)
    RING = 3
    adj_in = sb("ag_adj", [P, RING, CHUNK * P], I32)
    masked = sb("ag_masked", [P, RING, CHUNK * P], BF16)
    maskT = sb("ag_maskT", [P, RING, CHUNK, P], F32R)
    x_in = sb("ag_x", [P, D])
    self_in = sb("ag_self", [P, D])
    y = sb("ag_y", [P, D])
    degree = sb("ag_degree", [P, 2, CHUNKS])
    small = sb("ag_small", [P, 2])
    pT = ctx.enter_context(nc.psum_tensor("ag_pT", [P, RING, 2 * BANK], BF16))
    pA = ctx.enter_context(nc.psum_tensor("ag_pA", [P, 2, BANK], F32))
    adj_here = [m.sem(f"ag_adj_here{r}") for r in range(RING)]
    cleared, adj_masked, transposed, maskT_ready, stored_mask, multiplied, pA_read, rows_here, rows_used, y_ready, \
        y_stored, chain = m.sems("ag_",
            "cleared adj_masked transposed maskT_ready stored_mask multiplied pA_read rows_here "
            "rows_used y_ready y_stored chain")
    tiles_of = lambda c: min(CHUNK, T - c * CHUNK)
    with nc.Block() as block:
        @block.sync
        def _(sp):
            def load(t, p, left):
                for c in range(CHUNKS):
                    first, cols = c * CHUNK * P, min(CHUNK * P, N - c * CHUNK * P)
                    sp.wait_ge(adj_masked, t * CHUNKS + c + 1)
                    if not left:
                        sp.dma_start(adj_in[0:LAST, c % RING, 0:cols], adj[(T - 1) * P:N, first:first + cols])\
                          .then_inc(adj_here[c % RING], 16)
                    else:
                        full = adj[0:(T - 1) * P].rearrange("(t p) j -> t p j", p=P)
                        sp.dma_start(adj_in[:, c % RING, 0:cols], full[t][:, first:first + cols])\
                          .then_inc(adj_here[c % RING], 16)

            each_tile(sp, load)

        @block.gpsimd
        def _(pool):
            pool.memset(x_in[:], 0.0).then_inc(cleared, 1)

            def step(t, p, left):
                for c in range(CHUNKS):
                    pool.wait_ge(maskT_ready, t * CHUNKS + c + 1 + RING)
                    nc.gpsimd.tensor_copy(m.mask[:, c * CHUNK:c * CHUNK + tiles_of(c), bass.ts(t, P)],
                                          maskT[:, c % RING, 0:tiles_of(c)].bitcast(F32)).then_inc(stored_mask, 1)

            pool.sem_inc(stored_mask, RING)
            each_tile(pool, step)

        @block.scalar
        def _(act):
            def rows(t, last):
                act.wait_ge(rows_used, t + 1)
                if last:
                    act.dma_start(x_in[0:LAST], x[(T - 1) * P:N]).then_inc(rows_here, 16)
                else:
                    full = x[0:(T - 1) * P].rearrange("(t p) d -> t p d", p=P)
                    act.dma_start(x_in[:], full[t]).then_inc(rows_here, 16)
                act.dma_start(self_in[:], row_tile(m.self_part, t)).then_inc(rows_here, 16)

            def copy(t, c):
                n = t * CHUNKS + c
                act.wait_ge(transposed, n + 1 + RING)
                act.wait_ge(multiplied, n + 1)
                act.wait_ge(stored_mask, n + 1)
                k = tiles_of(c)
                nc.scalar.activation(maskT[:, c % RING, 0:k].rearrange("p c i -> p (c i)"), pT[:, c % RING, 0:k * P],
                                     ACT.Copy).then_inc(maskT_ready, 1)

            def step(t, p, left):
                for c in range(CHUNKS):
                    if left:
                        copy(t + 1, c)
                    if c == 5:
                        act.wait_ge(y_ready, t + 1)
                        act.dma_start(row_tile(m.y, t), y[:]).then_inc(y_stored, 16)
                    if c == 6 and left:
                        rows(t + 1, left == 1)

            act.sem_inc(maskT_ready, RING)
            act.wait_ge(cleared, 1)
            rows(0, False)
            for c in range(CHUNKS):
                copy(0, c)
            each_tile(act, step)
            act.wait_ge(y_stored, 16 * (T + 1))

        @block.tensor
        def _(pe):
            def transposes(t, c):
                n = t * CHUNKS + c
                pe.wait_ge(adj_masked, n + 1 + RING)
                pe.wait_ge(maskT_ready, n + 1)
                for k in range(tiles_of(c)):
                    last = nc.tensor.transpose(pT[:, c % RING, k * P:(k + 1) * P],
                                               masked[:, c % RING, k * P:(k + 1) * P], m.identb[:])
                last.then_inc(transposed, 1)

            def step(t, p, left):
                for c in range(CHUNKS):
                    if c + 1 < CHUNKS:
                        transposes(t, c + 1)
                    elif left:
                        transposes(t + 1, 0)
                    if c == 0:
                        pe.wait_ge(pA_read, t + 1)
                    pe.wait_ge(maskT_ready, t * CHUNKS + c + 1 + RING)
                    for k in range(tiles_of(c)):
                        j = c * CHUNK + k
                        for part in range(2):
                            last = nc.tensor.matmul(pA[:, p], maskT[:, c % RING, k], m.zs[:, j, part],
                                                    start=j == 0 and part == 0, stop=j == T - 1 and part == 1)
                    last.then_inc(multiplied, 1)

            pe.sem_inc(transposed, RING)
            pe.sem_inc(multiplied, RING)
            transposes(0, 0)
            each_tile(pe, step)

        @block.vector
        def _(dve):
            own = Chain(dve, chain)
            dve.sem_inc(adj_masked, RING)
            dve.sem_inc(pA_read, 2)
            dve.sem_inc(rows_used, 1)
            dve.sem_inc(y_stored, 16)

            def mask_rows(t, p, c):
                cols = min(CHUNK * P, N - c * CHUNK * P)
                dve.wait_ge(transposed, t * CHUNKS + c + 1)
                dve.wait_ge(adj_here[c % RING], (t * RING + c // RING + 1) * 16)
                if c == CHUNKS - 1:
                    nc.vector.memset(masked[:, c % RING, cols:tiles_of(c) * P], 0.0)
                nc.vector.tensor_scalar(masked[:, c % RING, 0:cols], adj_in[:, c % RING, 0:cols], 0.0, 0.0, ALU.is_gt,
                                        ALU.add, accum_out=degree[:, p, c:c + 1]).then_inc(adj_masked, 1)

            def finish(t, p):
                own.at(t * 5)
                dve.wait_ge(adj_masked, (t + 1) * CHUNKS + RING)
                own.link(nc.vector.tensor_reduce(small[:, 0:1], degree[:, p], AX, ALU.add))
                own.link(nc.vector.tensor_scalar(m.empty[:, bass.ts(t, 1)], small[:, 0:1], 0.0, None, ALU.is_equal))
                own.link(nc.vector.tensor_scalar(small[:, 0:1], small[:, 0:1], 1.0, None, ALU.max))
                own.link(nc.vector.reciprocal(small[:, 1:2], small[:, 0:1]))
                dve.wait_ge(multiplied, (t + 1) * CHUNKS + RING)
                dve.wait_ge(rows_here, (t + 1) * 32)
                nc.vector.scalar_tensor_tensor(out=self_in[:], in0=pA[:, p], scalar=small[:, 1:2], in1=self_in[:],
                                               op0=ALU.mult, op1=ALU.add).then_inc(pA_read, 1)
                dve.wait_ge(pA_read, t + 3)
                dve.wait_ge(y_stored, (t + 1) * 16)
                nc.vector.scalar_tensor_tensor(out=y[:], in0=self_in[:], scalar=0.0, in1=x_in[:],
                                               op0=ALU.max, op1=ALU.add).then_inc(y_ready, 1)
                dve.wait_ge(y_ready, t + 1)
                dve.sem_inc(rows_used, 1)
                own.link(nc.vector.bn_stats(m.stats[:, t], y[:]))

            def step(t, p, left):
                for c in range(CHUNKS):
                    if left:
                        mask_rows(t + 1, 1 - p, c)
                    if c == 3:
                        finish(t, p)

            for c in range(CHUNKS):
                mask_rows(0, 0, c)
            each_tile(dve, step)


def load_moments(nc, own, m, mean, rstd, work):
    st = m.stats
    v = nc.vector
    own.link(v.tensor_tensor(mean[:], st[:, :, 1], st[:, :, 4], ALU.add))
    own.link(v.tensor_tensor(work[:], st[:, :, 1], st[:, :, 4], ALU.subtract))
    own.link(v.tensor_scalar(mean[:], mean[:], 0.5, None, ALU.mult))
    own.link(v.tensor_scalar(work[:], work[:], 0.5, None, ALU.mult))
    own.link(v.tensor_tensor(work[:], work[:], work[:], ALU.mult))
    own.link(v.tensor_tensor(rstd[:], st[:, :, 2], st[:, :, 5], ALU.add))
    own.link(v.tensor_scalar(rstd[:], rstd[:], 1.0 / D, EPS, ALU.mult, ALU.add))
    own.link(v.tensor_tensor(work[:], work[:], rstd[:], ALU.add))


MOMENT_LINKS = 8


def project(nc, ctx, m, name, layer):
    H, b1, b2 = layer["H"], layer["b1"], layer["b2"]
    O = D // H
    PARTS = 2 if H > 1 else 1
    ROWS = H * T // PARTS
    sb = lambda n, s, d=F32: ctx.enter_context(nc.sbuf_tensor(f"{name}p_{n}", s, d))
    ps = lambda n, s: ctx.enter_context(nc.psum_tensor(f"{name}p_{n}", s, F32))
    W = sb("W", [P, C, D])
    a1, a2 = sb("a1", [P, H, O]), sb("a2", [P, H, O])
    b1_wide = sb("b1", [P, D])
    b2_wide = sb("b2", [P, 1])
    y_in, x_out = sb("y", [P, 2, D]), sb("x", [P, 2, D])
    W_high, W_low = sb("W_high", [P, C, D], F32R), sb("W_low", [P, C, D], F32R)
    xT_high, xT_low = sb("xT_high", [P, 2, C, P], F32R), sb("xT_low", [P, 2, C, P], F32R)
    h_out = sb("h", [P, 2, D])
    prod = sb("prod", [P, 2, D])
    h_sum = sb("h_sum", [P, D])
    f1, f2, R = sb("f1", [P, H, T]), sb("f2", [P, H, T]), sb("R", [P, H, T])
    f2_top, f2_max = sb("f2_top", [P, H]), sb("f2_max", [P, H])
    mean, rstd, shift, work = (sb(n, [P, T]) for n in ("mean", "rstd", "shift", "work"))
    over_n = sb("over_n", [P, P])
    rT = sb("rT", [P, 2, P])
    pT, pH = ps("pT", [P, 2, BANK]), ps("pH", [P, 2, BANK])
    pR, pM = ps("pR", [P, 2, BANK]), ps("pM", [P, BANK])
    y_here = [m.sem(f"{name}p_y_here{p}") for p in range(2)]
    x_stored = [m.sem(f"{name}p_x_stored{p}") for p in range(2)]
    h_stored = [m.sem(f"{name}p_h_stored{p}") for p in range(2)]
    W_here = [m.sem(f"{name}p_W_here{c}") for c in range(C)]
    loaded, W_cut, W_ready, var_ready, std_ready, moments_ready, x_ready, transposed, high_ready, xT_ready, projected, \
        h_ready, f_done, summed, sum_start, tops, maxed, args, exps, rowsT, rows_out, rows_stored, meaned, \
        chain = m.sems(f"{name}p_",
            "loaded W_cut W_ready var_ready std_ready moments_ready x_ready transposed high_ready "
            "xT_ready projected h_ready f_done summed sum_start tops maxed args exps rowsT rows_out "
            "rows_stored meaned chain")
    n_loads = 2 + (2 if b1 is not None else 0)
    with nc.Block() as block:
        @block.sync
        def _(sp):
            def load(t, p, left=2):
                sp.wait_ge(x_ready, t + 1)
                sp.dma_start(y_in[:, p], row_tile(m.y, t)).then_inc(y_here[p], 16)

            for t in range(2):
                load(t, t)
            for c in range(C):
                sp.dma_start(W[:, c].rearrange("p (h o) -> p h o", h=H) if H > 1 else W[:, c],
                             layer["W"][c * P:(c + 1) * P]).then_inc(W_here[c], 16)
            sp.dma_start(a1[:], layer["a1"].partition_broadcast(P)).then_inc(loaded, 16)
            sp.dma_start(a2[:], layer["a2"].partition_broadcast(P)).then_inc(loaded, 16)
            if b1 is not None:
                sp.dma_start(b1_wide[:], b1.partition_broadcast(P)).then_inc(loaded, 16)
                sp.dma_start(b2_wide[:], b2.partition_broadcast(P)).then_inc(loaded, 16)

            with sp.Fori(0, T // 2 - 1) as pair:
                for p in range(2):
                    load(pair * 2 + 2 + p, p)
            for q in range(PARTS):
                sp.wait_ge(rows_out, q + 1)
                heads = m.rows[q * (H // PARTS):(q + 1) * (H // PARTS)]
                sp.dma_start(heads.rearrange("h (t p) -> (h t) p", p=P), rT[0:ROWS, q]).then_inc(rows_stored, 16)
            sp.wait_ge(rows_stored, 16 * PARTS)

        @block.gpsimd
        def _(pool):
            own = Chain(pool, summed)
            nc.gpsimd.memset(h_sum[:], 0.0).then_inc(sum_start, 1)
            pool.wait_ge(sum_start, 1)

            def step(t, p, left):
                pool.wait_ge(h_ready, t + 3)
                own.at(t + 2)
                rows = P if left else LAST
                own.link(nc.gpsimd.tensor_tensor(h_sum[0:rows], h_sum[0:rows], h_out[0:rows, p], ALU.add))

            each_tile(pool, step)
            pool.wait_ge(tops, 1)
            nc.gpsimd.partition_all_reduce(f2_max[:], f2_top[:], P, RMAX).then_inc(maxed, 1)

        @block.tensor
        def _(pe):
            def transposes(t, p):
                pe.wait_ge(x_ready, t + 3)
                pe.wait_ge(xT_ready, t + 1)
                for c in range(C):
                    last = nc.tensor.transpose(pT[:, p, c * P:(c + 1) * P], x_out[:, p, c * P:(c + 1) * P], m.ident[:])
                last.then_inc(transposed, 1)

            def step(t, p, left):
                pe.wait_ge(xT_ready, t + 3)
                pe.wait_ge(h_ready, t + 1)
                product_in_parts(nc, pH[:, p], xT_high[:, p], xT_low[:, p], W_high, W_low).then_inc(projected, 1)
                if left >= 2:
                    transposes(t + 2, p)

            transposes(0, 0)
            transposes(1, 1)
            pe.wait_ge(W_ready, C)
            each_tile(pe, step)
            pe.wait_ge(summed, T + 2)
            nc.tensor.matmul(pM[:], over_n[:], h_sum[:], start=True, stop=True).then_inc(meaned, 1)
            pe.wait_ge(exps, 3)
            flat = R[:].rearrange("p h t -> p (h t)")
            for q in range(PARTS):
                nc.tensor.transpose(pR[0:ROWS, q, 0:P], flat[:, q * ROWS:(q + 1) * ROWS], m.ident[:]).then_inc(rowsT, 1)

        @block.scalar
        def _(act):
            act.wait_ge(var_ready, 1)
            nc.scalar.activation(work[:], work[:], ACT.Sqrt).then_inc(std_ready, 1)

            def normalise(t, p):
                act.wait_ge(y_here[p], (t - p) * 8 + 16)
                act.wait_ge(transposed, t + 1)
                act.wait_ge(x_stored[p], (t - p) * 8 + 16)
                nc.scalar.activation(x_out[:, p], y_in[:, p], ACT.Identity, scale=rstd[:, bass.ts(t, 1)],
                                     bias=shift[:, bass.ts(t, 1)]).then_inc(x_ready, 1)
                act.wait_ge(x_ready, t + 3)
                act.dma_start(row_tile(m.x, t), x_out[:, p]).then_inc(x_stored[p], 16)

            def copy_xT(t, p):
                act.wait_ge(transposed, t + 3)
                act.wait_ge(projected, t + 1)
                nc.scalar.activation(xT_high[:, p].rearrange("p c i -> p (c i)"), pT[:, p], ACT.Copy).then_inc(high_ready, 1)

            def step(t, p, left):
                if left >= 2:
                    normalise(t + 2, p)
                if b1 is None:
                    act.wait_ge(projected, t + 3)
                    act.wait_ge(f_done, t * 2 + 2)
                    act.wait_ge(summed, t + 1)
                    act.wait_ge(h_stored[p], (t - p) * 8 + 16)
                    nc.scalar.activation(h_out[:, p], pH[:, p], ACT.Copy).then_inc(h_ready, 1)
                if left >= 2:
                    copy_xT(t + 2, p)
                act.wait_ge(h_ready, t + 3)
                act.dma_start(row_tile(m.h, t), h_out[:, p]).then_inc(h_stored[p], 16)

            act.wait_ge(moments_ready, 1)
            for t in range(2):
                normalise(t, t)
            for c in range(C):
                act.wait_ge(W_here[c], 16)
                nc.scalar.activation(W_high[:, c], W[:, c], ACT.Copy).then_inc(W_cut, 1)
                if c % 2:
                    copy_xT(c // 2, c // 2)
            each_tile(act, step)
            for p in range(2):
                act.wait_ge(x_stored[p], 16 * (T // 2 + 1))
                act.wait_ge(h_stored[p], 16 * (T // 2 + 1))
            for n, t in enumerate((m.b, m.u, R)):
                act.wait_ge(args, n + 1)
                nc.scalar.activation(t[:, 0:H], t[:, 0:H], ACT.Exp).then_inc(exps, 1)

        @block.vector
        def _(dve):
            v = nc.vector
            own = Chain(dve, chain)
            own.link(v.memset(over_n[:], 1.0 / N))
            dve.sem_inc(x_ready, 2)
            dve.sem_inc(projected, 2)
            dve.sem_inc(transposed, 2)
            dve.sem_inc(h_ready, 2)
            dve.sem_inc(f_done, 4)
            dve.sem_inc(summed, 2)
            for p in range(2):
                dve.sem_inc(x_stored[p], 16)
                dve.sem_inc(h_stored[p], 16)

            load_moments(nc, own, m, mean, rstd, work)
            dve.sem_inc(var_ready, 1)
            dve.wait_ge(std_ready, 1)
            own.link(v.reciprocal(rstd[:], work[:]))
            v.scalar_tensor_tensor(out=shift[:], in0=mean[:], scalar=-1.0, in1=rstd[:], op0=ALU.mult,
                                   op1=ALU.mult).then_inc(moments_ready, 1)
            dve.sem_inc(xT_ready, 2)
            before = MOMENT_LINKS + 2

            def cut_xT(t, p):
                dve.wait_ge(high_ready, t + 1)
                flat = lambda a: a[:, p].rearrange("p c i -> p (c i)")
                v.tensor_tensor(flat(xT_low), pT[:, p], flat(xT_high).bitcast(F32), ALU.subtract).then_inc(xT_ready, 1)

            for c in range(C):
                dve.wait_ge(W_cut, c + 1)
                v.tensor_tensor(W_low[:, c], W[:, c], W_high[:, c].bitcast(F32), ALU.subtract).then_inc(W_ready, 1)
                if c % 2:
                    cut_xT(c // 2, c // 2)
            dve.wait_ge(loaded, 16 * n_loads)

            def step(t, p, left):
                if b1 is not None:
                    dve.wait_ge(projected, t + 3)
                    dve.wait_ge(summed, t + 1)
                    dve.wait_ge(h_stored[p], (t - p) * 8 + 16)
                    v.tensor_tensor(h_out[:, p], pH[:, p], b1_wide[:], ALU.add).then_inc(h_ready, 1)
                if left >= 2:
                    cut_xT(t + 2, p)
                dve.wait_ge(h_ready, t + 3)
                own.at(t * 2 + before)
                flat = lambda a: a[:].rearrange("p h o -> p (h o)")
                dve.wait_ge(f_done, t * 2 + 4)
                if H == 1:
                    for n, (a, f) in enumerate(((a1, f1), (a2, f2))):
                        v.scalar_tensor_tensor(out=prod[:, n], in0=h_out[:, p], scalar=1.0, in1=flat(a), op0=ALU.mult,
                                               op1=ALU.mult, accum_out=f[:, 0, bass.ts(t, 1)]).then_inc(f_done, 1)
                    return
                own.link(v.tensor_tensor(prod[:, 0], h_out[:, p], flat(a1), ALU.mult))
                own.link(v.tensor_tensor(prod[:, 1], h_out[:, p], flat(a2), ALU.mult))
                for n, f in enumerate((f1, f2)):
                    v.tensor_reduce(f[:, :, t], prod[:, n].rearrange("p (h o) -> p h o", h=H), AX,
                                    ALU.add).then_inc(f_done, 1)

            each_tile(dve, step)
            own.at((T * 2 if H > 1 else 0) + before)
            dve.wait_ge(f_done, 2 * T + 4)
            v.tensor_reduce(f2_top[:], f2[:], AX, ALU.max).then_inc(tops, 1)
            dve.wait_ge(maxed, 1)
            wide = lambda a: a[:].rearrange("p (h o) -> p h o", o=1).broadcast_to([P, H, T])
            own.link(v.tensor_tensor(f2[:], f2[:], wide(f2_max), ALU.subtract))
            v.tensor_scalar(m.b[:, 0:H], f2[:], B_SHIFT, None, ALU.add).then_inc(args, 1)
            v.tensor_scalar(m.u[:, 0:H], f2[:], -(1 - SLOPE), -U_SHIFT, ALU.mult, ALU.add).then_inc(args, 1)
            own.link(v.tensor_tensor(f1[:], f1[:], wide(f2_max), ALU.add))
            if b2 is not None:
                own.link(v.tensor_scalar(f1[:], f1[:], b2_wide[:], None, ALU.add))
            own.link(v.tensor_scalar(f1[:], f1[:], 1 - SLOPE, -U_SHIFT, ALU.mult, ALU.add))
            v.tensor_scalar(R[:], f1[:], R_TOP, None, ALU.min).then_inc(args, 1)
            dve.wait_ge(meaned, 1)
            v.tensor_copy(m.mean_h[:], pM[:])
            for q in range(PARTS):
                dve.wait_ge(rowsT, q + 1)
                v.tensor_copy(rT[0:ROWS, q], pR[0:ROWS, q, 0:P]).then_inc(rows_out, 1)


def attend_one_head(nc, ctx, m, name):
    sb = lambda n, s, d=F32: ctx.enter_context(nc.sbuf_tensor(f"{name}a_{n}", s, d))
    W = 2 * P
    CH = T // 2
    HALF = D // 2
    R = sb("R", [P, 2, W])
    V_high = sb("V_high", [P, T, D + 2], F32R)
    V_low = sb("V_low", [P, T, D + 2], F32R)
    weights = sb("weights", [P, 2, W])
    w_high = sb("w_high", [P, 2, W], F32R)
    w_low = sb("w_low", [P, 2, W], F32R)
    rows = sb("rows", [P, 2, D])
    neg = sb("neg", [P, D])
    rden = sb("rden", [P, 2])
    acc = ctx.enter_context(nc.psum_tensor(f"{name}a_acc", [P, 2, 2, 2, BANK], F32))
    v_here, r_here, x_here, y_stored = ([m.sem(f"{name}a_{n}{p}") for p in range(2)] for n in (
        "v_here", "r_here", "x_here", "y_stored"))
    b_cut, v_cut, v_ready, w_ready, high_ready, low_ready, w_used, dens, scaled, shared, negated, exped, lifted, y_ready, \
        counted = m.sems(f"{name}a_",
            "b_cut v_cut v_ready w_ready high_ready low_ready w_used dens scaled shared negated "
            "exped lifted y_ready counted")

    def later_chunks(eng, body):
        with eng.Fori(0, (CH - 1) // 2) as pair:
            for q in range(2):
                body(pair * 2 + 1 + q, (1 + q) % 2)

    halves = lambda a: a.rearrange("p (b n) -> p b n", b=2)

    def share(cp, i):
        return acc[:, cp, i, :, 0:HALF]

    with nc.Block() as block:
        @block.sync
        def _(sp):
            def load_R(c, cp):
                sp.dma_start(R[:, cp], m.rows[0][bass.ts(c, W)].partition_broadcast(P)).then_inc(r_here[cp], 16)

            def load_h(j, p, left):
                sp.wait_ge(v_ready, j + 1)
                sp.dma_start(rows[:, p], row_tile(m.h, j)).then_inc(v_here[p], 16)

            def load_x(t, p):
                sp.wait_ge(y_stored[p], (t - p) * 8 + 16)
                sp.dma_start(rows[:, p], row_tile(m.x, t)).then_inc(x_here[p], 16)

            def chunk(c, cp):
                sp.wait_ge(w_ready, (c - 1) * T + 1)
                load_R(c, cp)
                for i in range(2):
                    load_x((c - 1) * 2 + i, i)

            load_R(0, 0)
            each_tile(sp, load_h)
            sp.wait_ge(v_ready, T + 2)
            later_chunks(sp, chunk)
            for i in range(2):
                load_x((CH - 1) * 2 + i, i)

        @block.scalar
        def _(act):
            def cut_values(j):
                act.wait_ge(v_here[j % 2], (j // 2 + 1) * 16)
                nc.scalar.activation(V_high[:, j, 0:D], rows[:, j % 2], ACT.Copy,
                                     scale=m.b[:, 0, j:j + 1]).then_inc(v_cut, 1)

            def cut_weights(c, j):
                act.wait_ge(w_ready, c * T + j + 1)
                act.wait_ge(w_used, c * T + j + 1)
                nc.scalar.activation(w_high[:, j % 2], weights[:, j % 2], ACT.Copy).then_inc(high_ready, 1)

            def negate(t, cp, i):
                act.wait_ge(shared, t + 1)
                act.wait_ge(y_ready, t + 1)
                nc.scalar.activation(halves(neg[:]), share(cp, i), ACT.Relu, scale=-1.0).then_inc(negated, 1)

            def exponential(t):
                act.wait_ge(negated, t + 1)
                nc.scalar.activation(neg[:], neg[:], ACT.Exp, scale=-1.0).then_inc(exped, 1)

            def store_y(t, i):
                act.wait_ge(counted, t + 1)
                act.dma_start(row_tile(m.y, t), rows[:, i]).then_inc(y_stored[i], 16)

            def chunk(c, cp):
                for j in range(T):
                    cut_weights(c, j)
                    for i in range(2):
                        t, at = (c - 1) * 2 + i, j - 11 * i
                        if at == 6:
                            negate(t, 1 - cp, i)
                        if at == 7:
                            exponential(t)
                        if at == 13:
                            store_y(t, i)

            act.sem_inc(high_ready, 2)
            cut_values(0)
            for j in range(T):
                if j + 1 < T:
                    cut_values(j + 1)
                cut_weights(0, j)
            later_chunks(act, chunk)
            for i in range(2):
                negate((CH - 1) * 2 + i, (CH - 1) % 2, i)
                exponential((CH - 1) * 2 + i)
                store_y((CH - 1) * 2 + i, i)
            for i in range(2):
                act.wait_ge(y_stored[i], 16 * (CH + 1))

        @block.tensor
        def _(pe):
            def chunk(c, cp, first=False):
                if not first:
                    pe.wait_ge(lifted, c * 2)
                for j in range(T):
                    if first:
                        pe.wait_ge(v_ready, j + 3)
                    for part, w_part, ready in ((0, w_high, high_ready), (1, w_low, low_ready)):
                        pe.wait_ge(ready, c * T + j + 3)
                        for i in range(2):
                            w = w_part[:, j % 2, i * P:(i + 1) * P]
                            for values in (V_high, V_low)[:2 - part]:
                                starts, ends = j == 0 and values is V_high and part == 0, j == T - 1 and part == 1
                                nc.tensor.matmul(acc[:, cp, i, 0, 0:HALF], w, values[:, j, 0:HALF],
                                                 start=starts, stop=ends)
                                last = nc.tensor.matmul(acc[:, cp, i, 1, 0:HALF + 2], w, values[:, j, HALF:D + 2],
                                                        start=starts, stop=ends)
                    last.then_inc(w_used, 1)

            pe.sem_inc(w_used, 2)
            pe.wait_ge(b_cut, 2)
            chunk(0, 0, first=True)
            later_chunks(pe, chunk)

        @block.vector
        def _(dve):
            v = nc.vector
            dve.sem_inc(v_ready, 2)
            for p in range(2):
                dve.sem_inc(y_stored[p], 16)
            dve.sem_inc(low_ready, 2)
            dve.sem_inc(lifted, 2)
            dve.sem_inc(y_ready, 1)
            b = m.b[:, 0].rearrange("p (t o) -> p t o", o=1).broadcast_to([P, T, 2])
            v.tensor_copy(V_high[:, :, D:D + 2], b).then_inc(b_cut, 1)
            dve.wait_ge(b_cut, 1)
            v.tensor_tensor(V_low[:, :, D:D + 2], b, V_high[:, :, D:D + 2].bitcast(F32), ALU.subtract).then_inc(b_cut, 1)

            def make(c, cp, j):
                if j == 0:
                    dve.wait_ge(r_here[cp], (c - cp) * 8 + 16)
                dve.wait_ge(high_ready, c * T + j + 1)
                dve.wait_ge(low_ready, c * T + j + 1)
                v.scalar_tensor_tensor(out=weights[:, j % 2], in0=R[:, cp], scalar=m.u[:, 0, j:j + 1],
                                       in1=m.mask[:, j, bass.ts(c, W)], op0=ALU.max, op1=ALU.mult).then_inc(w_ready, 1)

            def cut_weights(c, j):
                dve.wait_ge(high_ready, c * T + j + 3)
                dve.wait_ge(w_used, c * T + j + 1)
                v.tensor_tensor(w_low[:, j % 2], weights[:, j % 2], w_high[:, j % 2].bitcast(F32),
                                ALU.subtract).then_inc(low_ready, 1)

            def cut_values(j):
                dve.wait_ge(v_cut, j + 1)
                v.scalar_tensor_tensor(out=V_low[:, j, 0:D], in0=rows[:, j % 2], scalar=m.b[:, 0, j:j + 1],
                                       in1=V_high[:, j, 0:D].bitcast(F32), op0=ALU.mult,
                                       op1=ALU.subtract).then_inc(v_ready, 1)

            def invert(t, cp, i):
                dve.wait_ge(w_used, (t - i) * (T // 2) + T + 2)
                v.tensor_scalar(rden[:, i:i + 1], acc[:, cp, i, 1, HALF:HALF + 1], m.empty[:, bass.ts(t, 1)], None,
                                ALU.add).then_inc(dens, 1)
                dve.wait_ge(dens, t * 2 + 1)
                v.reciprocal(rden[:, i:i + 1], rden[:, i:i + 1]).then_inc(dens, 1)

            def scale(t, cp, i):
                dve.wait_ge(dens, t * 2 + 2)
                v.tensor_scalar(share(cp, i), share(cp, i), rden[:, i:i + 1], None, ALU.mult).then_inc(scaled, 1)

            def mean(t, cp, i):
                dve.wait_ge(scaled, t + 1)
                v.scalar_tensor_tensor(out=share(cp, i), in0=halves(m.mean_h[:]), scalar=m.empty[:, bass.ts(t, 1)],
                                       in1=share(cp, i), op0=ALU.mult, op1=ALU.add).then_inc(shared, 1)

            def lift(t, cp, i):
                dve.wait_ge(exped, t + 1)
                v.scalar_tensor_tensor(out=halves(neg[:]), in0=share(cp, i), scalar=0.0, in1=halves(neg[:]), op0=ALU.max,
                                       op1=ALU.add).then_inc(lifted, 1)

            def residual(t, cp, i):
                dve.wait_ge(lifted, t + 3)
                dve.wait_ge(x_here[i], (t - i) * 8 + 16)
                v.scalar_tensor_tensor(out=rows[:, i], in0=neg[:], scalar=-1.0, in1=rows[:, i], op0=ALU.add,
                                       op1=ALU.add).then_inc(y_ready, 1)

            def count(t, cp, i):
                dve.wait_ge(y_ready, t + 2)
                v.bn_stats(m.stats[:, t], rows[:, i]).then_inc(counted, 1)

            finish = {2: invert, 3: scale, 4: mean, 9: lift, 10: residual, 11: count}

            def chunk(c, cp):
                for j in range(T):
                    make(c, cp, j)
                    cut_weights(c, j - 1)
                    for i in range(2):
                        if j - 11 * i in finish:
                            finish[j - 11 * i]((c - 1) * 2 + i, 1 - cp, i)

            for j in range(T):
                make(0, 0, j)
                cut_values(j)
                if j > 0:
                    cut_weights(0, j - 1)
            later_chunks(dve, chunk)
            cut_weights(CH - 1, T - 1)
            for i in range(2):
                for step in finish.values():
                    step((CH - 1) * 2 + i, (CH - 1) % 2, i)


def attend_heads(nc, ctx, m, name, H):
    O = D // H
    PER, PICK = 5, (1, 3)
    GROUPS = T // PER
    split = [PER * g + q for g in range(GROUPS) for q in PICK]
    HALF, BANKS, RING = NP // 2, 4, 4
    WIDTH = HALF // BANKS
    UNITS = 2 * H
    sb = lambda n, s, d=F32: ctx.enter_context(nc.sbuf_tensor(f"{name}a_{n}", s, d))
    R = sb("R", [P, 2, HALF])
    V = sb("V", [P, 2, T, O + 1])
    V_high = sb("V_high", [P, 2, len(split), O + 1], F32R)
    V_low = sb("V_low", [P, 2, len(split), O + 1], F32R)
    weights = sb("weights", [P, RING, HALF])
    w_high = sb("w_high", [P, 2, HALF], F32R)
    w_low = sb("w_low", [P, 2, HALF], F32R)
    sums = sb("sums", [P, HALF])
    acc = ctx.enter_context(nc.psum_tensor(f"{name}a_acc", [P, 2, BANKS, BANK], F32))
    r_here = [m.sem(f"{name}a_r_here{p}") for p in range(2)]
    v_here = [m.sem(f"{name}a_v_here{p}") for p in range(2)]
    v_scaled, v_cut, v_ready, w_ready, w_used, high_ready, low_ready, evacuated, stored = m.sems(f"{name}a_",
            "v_scaled v_cut v_ready w_ready w_used high_ready low_ready evacuated stored")

    def each_unit(eng, body):
        with eng.Fori(0, H // 2) as pair:
            for hp in range(2):
                for half in range(2):
                    h = pair * 2 + hp
                    body(h * 2 + half, h, half, hp)

    nums = m.num.rearrange("(s t) h o n -> s h o t n", s=2)
    dens = m.den.rearrange("(s t) (h a) n -> s h a t n", s=2, a=1)

    def cut_parts(p, q):
        high, low = (a[:, p].rearrange("p (g f) o -> p g f o", f=len(PICK))[:, :, q] for a in (V_high, V_low))
        return V[:, p, 0:PER * GROUPS].rearrange("p (g f) o -> p g f o", f=PER)[:, :, PICK[q]], high, low

    with nc.Block() as block:
        @block.sync
        def _(sp):
            values = m.h.rearrange("(t p) (h o) -> h p t o", p=P, h=H)

            def load(n, h, half, hp):
                if half == 0:
                    sp.wait_ge(w_used, (n + 2) * T)
                    sp.dma_start(V[:, hp, :, 0:O], values[h]).then_inc(v_here[hp], 16)
                sp.wait_ge(w_ready, (n + 1) * T)
                sp.dma_start(R[:, half], m.rows[h][half * HALF:(half + 1) * HALF].partition_broadcast(P))\
                  .then_inc(r_here[half], 16)

            each_unit(sp, load)

        @block.gpsimd
        def _(pool):
            with pool.Fori(0, H // 2) as pair:
                for hp in range(2):
                    for q in range(len(PICK)):
                        whole, high, low = cut_parts(hp, q)
                        pool.wait_ge(v_cut, (pair * 2 + hp) * len(PICK) + q + 1)
                        nc.gpsimd.tensor_tensor(low, whole, high.bitcast(F32), ALU.subtract).then_inc(v_ready, 1)

        @block.vector
        def _(dve):
            dve.sem_inc(w_ready, 2 * T)

            def unit(n, h, half, hp):
                def cut(j):
                    s = split.index(j)
                    dve.wait_ge(high_ready, n * len(split) + s + 1)
                    nc.vector.tensor_tensor(w_low[:, s % 2], weights[:, (half * T + j) % RING],
                                            w_high[:, s % 2].bitcast(F32), ALU.subtract).then_inc(low_ready, 1)

                dve.wait_ge(r_here[half], h * 16 + 16)
                for j in range(T):
                    dve.wait_ge(w_used, (n + 4) * T + j + 1 - RING)
                    nc.vector.scalar_tensor_tensor(out=weights[:, (half * T + j) % RING], in0=R[:, half],
                                                   scalar=m.u[:, h, j:j + 1],
                                                   in1=m.mask[:, j, half * HALF:(half + 1) * HALF],
                                                   op0=ALU.max, op1=ALU.mult).then_inc(w_ready, 1)
                    if j - 1 in split:
                        cut(j - 1)

            each_unit(dve, unit)

        @block.tensor
        def _(pe):
            pe.sem_inc(w_used, 4 * T)

            def unit(n, h, half, hp):
                if half == 0:
                    pe.wait_ge(v_ready, (h + 1) * len(PICK))
                pe.wait_ge(evacuated, (n + 1) * BANKS)
                for j in range(T):
                    if j in split:
                        s = split.index(j)
                        pe.wait_ge(low_ready, n * len(split) + s + 1)
                        products = [(V_high[:, hp, s], w_high[:, s % 2]), (V_low[:, hp, s], w_high[:, s % 2]),
                                    (V_high[:, hp, s], w_low[:, s % 2])]
                    else:
                        pe.wait_ge(w_ready, (n + 2) * T + j + 1)
                        products = [(V[:, hp, j], weights[:, (half * T + j) % RING])]
                    for v, w in products:
                        for k in range(BANKS):
                            last = nc.tensor.matmul(acc[0:O + 1, half, k, 0:WIDTH], v, w[:, k * WIDTH:(k + 1) * WIDTH],
                                                    start=j == 0, stop=j == T - 1)
                    last.then_inc(w_used, 1)

            each_unit(pe, unit)

        @block.scalar
        def _(act):
            act.sem_inc(evacuated, 2 * BANKS)
            act.sem_inc(stored, 32)

            def evacuate(n, h, half):
                act.wait_ge(stored, n * 32 + 32)
                act.wait_ge(w_used, (n + 5) * T)
                for k in range(BANKS):
                    nc.scalar.activation(sums[0:O + 1, k * WIDTH:(k + 1) * WIDTH], acc[0:O + 1, half, k, 0:WIDTH],
                                         ACT.Copy).then_inc(evacuated, 1)
                act.wait_ge(evacuated, (n + 3) * BANKS)
                tiles = sums[:].rearrange("o (t n) -> o t n", n=P)
                act.dma_start(nums[half][h], tiles[0:O]).then_inc(stored, 16)
                act.dma_start(dens[half][h], tiles[O:O + 1]).then_inc(stored, 16)

            def scale_values(h, hp, tiles):
                for j in tiles:
                    if j == 0:
                        act.wait_ge(v_here[hp], (h - hp) * 8 + 16)
                        nc.scalar.activation(V[:, hp, :, O:O + 1], m.b[:, h].rearrange("p (t o) -> p t o", o=1),
                                             ACT.Copy).then_inc(v_scaled, 1)
                    nc.scalar.activation(V[:, hp, j, 0:O], V[:, hp, j, 0:O], ACT.Copy,
                                         scale=m.b[:, h, j:j + 1]).then_inc(v_scaled, 1)

            def cut_values(h, hp):
                act.wait_ge(v_scaled, (h + 1) * (T + 1))
                for q in range(len(PICK)):
                    whole, high, _ = cut_parts(hp, q)
                    nc.scalar.activation(high, whole, ACT.Copy).then_inc(v_cut, 1)

            def unit(n, h, half, hp):
                first, last = isinstance(n, int) and n == 0, isinstance(n, int) and n == UNITS - 1
                for s, j in enumerate(split):
                    if s == 2 and not first:
                        evacuate(n - 1, h - 1 if half == 0 else h, 1 - half)
                    if half == 1 and not last:
                        if 3 <= s < 9:
                            scale_values(h + 1, 1 - hp, range((s - 3) * T // 6, (s - 2) * T // 6))
                        if s == 9:
                            cut_values(h + 1, 1 - hp)
                    act.wait_ge(w_ready, (n + 2) * T + j + 1)
                    act.wait_ge(w_used, (n + (4 if s >= 2 else 3)) * T + split[s - 2] + 1)
                    nc.scalar.activation(w_high[:, s % 2], weights[:, (half * T + j) % RING],
                                         ACT.Copy).then_inc(high_ready, 1)

            scale_values(0, 0, range(T))
            cut_values(0, 0)
            for n in range(3):
                unit(n, n // 2, n % 2, n // 2 % 2)
            with act.Fori(0, (UNITS - 4) // 4) as four:
                for n in range(3, 7):
                    unit(four * 4 + n, four * 2 + n // 2, n % 2, n // 2 % 2)
            unit(UNITS - 1, H - 1, 1, 1)
            evacuate(UNITS - 1, H - 1, 1)
            act.wait_ge(stored, UNITS * 32 + 32)


def finish_heads(nc, ctx, m, name, H, elu, out):
    O = D // H
    sb = lambda n, s, d=F32: ctx.enter_context(nc.sbuf_tensor(f"{name}f_{n}", s, d))
    num = sb("num", [P, 2, C, P])
    den = sb("den", [H, 2, P])
    rden = sb("rden", [P, 2, H])
    share = sb("share", [P, 2, D])
    neg = sb("neg", [P, 2, D])
    x_in = sb("x_in", [P, 2, D])
    y = sb("y", [P, 2, D])
    mean, spread, squares, std, rstd = (sb(n, [P, 2]) for n in ("mean", "spread", "squares", "std", "rstd"))
    x_out = sb("x_out", [P, 2, D])
    pN = ctx.enter_context(nc.psum_tensor(f"{name}f_pN", [P, 2, BANK], F32))
    pD = ctx.enter_context(nc.psum_tensor(f"{name}f_pD", [P, 2, BANK], F32))
    here, x_here, stored = ([m.sem(f"{name}f_{n}{p}") for p in range(2)] for n in ("here", "x_here", "stored"))
    turned, dens, scaled, shared, negated, exped, lifted, y_ready, counted, halves, var_ready, std_ready, inverted, \
        normal = m.sems(f"{name}f_",
            "turned dens scaled shared negated exped lifted y_ready counted halves var_ready "
            "std_ready inverted normal")
    with nc.Block() as block:
        @block.sync
        def _(sp):
            pairs = m.num.rearrange("t (c a) o n -> t (a o) c n", a=P // O)

            def load_sums(t, p):
                sp.wait_ge(turned, t + 1)
                sp.dma_start(num[:, p], pairs[t]).then_inc(here[p], 16)
                sp.dma_start(den[:, p], m.den[t]).then_inc(here[p], 16)

            def load(t, p, left):
                if left:
                    load_sums(t + 1, 1 - p)
                sp.wait_ge(y_ready, t + 1)
                sp.dma_start(x_in[:, p], row_tile(m.x, t)).then_inc(x_here[p], 16)

            load_sums(0, 0)
            each_tile(sp, load)

        @block.tensor
        def _(pe):
            pe.sem_inc(turned, 2)

            def turn(t, p, left):
                pe.wait_ge(here[p], (t - p) * 16 + 32)
                pe.wait_ge(scaled, t + 1)
                for c in range(C):
                    nc.tensor.transpose(pN[:, p, c * P:(c + 1) * P], num[:, p, c], m.ident[:])
                nc.tensor.transpose(pD[:, p, 0:H], den[:, p], m.ident[0:H, 0:H]).then_inc(turned, 1)

            each_tile(pe, turn)

        @block.scalar
        def _(act):
            def step(t, p, left):
                if elu:
                    act.wait_ge(shared, t + 1)
                    act.wait_ge(y_ready, t + 1)
                    nc.scalar.activation(neg[:, p], share[:, p], ACT.Relu, scale=-1.0).then_inc(negated, 1)
                    act.wait_ge(negated, t + 1)
                    nc.scalar.activation(neg[:, p], neg[:, p], ACT.Exp, scale=-1.0).then_inc(exped, 1)
                if out is None:
                    return
                act.wait_ge(var_ready, t + 1)
                nc.scalar.activation(std[:, p:p + 1], std[:, p:p + 1], ACT.Sqrt).then_inc(std_ready, 1)
                act.wait_ge(normal, t + 1)
                if left:
                    act.dma_start(out[0:(T - 1) * P].rearrange("(t p) d -> t p d", p=P)[t],
                                  x_out[:, p]).then_inc(stored[p], 16)
                else:
                    act.dma_start(out[(T - 1) * P:N], x_out[0:LAST, p]).then_inc(stored[p], 16)

            if out is not None:
                each_tile(act, step)
                for p in range(2):
                    act.wait_ge(stored[p], 16 * (T // 2 + 1))
                return

            def store_y(t, p):
                act.wait_ge(y_ready, t + 3)
                act.dma_start(row_tile(m.y, t), y[:, p]).then_inc(stored[p], 16)

            step(0, 0, 2)
            with act.Fori(0, T // 2 - 1) as pair:
                for q in (1, 0):
                    step(pair * 2 + 2 - q, q, 2)
                    store_y(pair * 2 + 1 - q, 1 - q)
            step(T - 1, 1, 0)
            for p in range(2):
                store_y(T - 2 + p, p)
            for p in range(2):
                act.wait_ge(stored[p], 16 * (T // 2 + 1))

        @block.vector
        def _(dve):
            v = nc.vector
            heads = lambda a: a.rearrange("p (h o) -> p h o", h=H)
            dve.sem_inc(y_ready, 2)
            dve.sem_inc(scaled, 2)
            for p in range(2):
                dve.sem_inc(stored[p], 16)

            def add_empty(t, p):
                dve.wait_ge(turned, t + 3)
                v.tensor_scalar(rden[:, p], pD[:, p, 0:H], m.empty[:, bass.ts(t, 1)], None, ALU.add).then_inc(dens, 1)

            def invert(t, p):
                dve.wait_ge(dens, t * 2 + 1)
                v.reciprocal(rden[:, p], rden[:, p]).then_inc(dens, 1)

            def scale(t, p):
                dve.wait_ge(dens, t * 2 + 2)
                v.tensor_tensor(heads(share[:, p]), heads(pN[:, p]),
                                rden[:, p].rearrange("p (h o) -> p h o", o=1).broadcast_to([P, H, O]),
                                ALU.mult).then_inc(scaled, 1)

            def add_mean(t, p):
                dve.wait_ge(scaled, t + 3)
                v.scalar_tensor_tensor(out=share[:, p], in0=m.mean_h[:], scalar=m.empty[:, bass.ts(t, 1)], in1=share[:, p],
                                       op0=ALU.mult, op1=ALU.add).then_inc(shared, 1)

            def lift(t, p):
                dve.wait_ge(exped, t + 1)
                v.scalar_tensor_tensor(out=neg[:, p], in0=share[:, p], scalar=0.0, in1=neg[:, p], op0=ALU.max,
                                       op1=ALU.add).then_inc(lifted, 1)

            def residual(t, p):
                dve.wait_ge(x_here[p], (t - p) * 8 + 16)
                if elu:
                    dve.wait_ge(stored[p], (t - p) * 8 + 16)
                    dve.wait_ge(lifted, t + 1)
                    ins = v.scalar_tensor_tensor(out=y[:, p], in0=neg[:, p], scalar=-1.0, in1=x_in[:, p],
                                                 op0=ALU.add, op1=ALU.add)
                else:
                    dve.wait_ge(shared, t + 1)
                    ins = v.tensor_tensor(y[:, p], share[:, p], x_in[:, p], ALU.add)
                ins.then_inc(y_ready, 1)

            def count(t, p):
                dve.wait_ge(y_ready, t + 3)
                v.bn_stats(m.stats[:, t], y[:, p]).then_inc(counted, 1)

            def sums_of_halves(t, p):
                st, one = m.stats[:, t], slice(p, p + 1)
                dve.wait_ge(counted, t + 1)
                v.tensor_tensor(mean[:, one], st[:, 1:2], st[:, 4:5], ALU.add).then_inc(halves, 1)
                v.tensor_tensor(spread[:, one], st[:, 1:2], st[:, 4:5], ALU.subtract).then_inc(halves, 1)
                v.tensor_tensor(squares[:, one], st[:, 2:3], st[:, 5:6], ALU.add).then_inc(halves, 1)

            def moments(t, p):
                one = slice(p, p + 1)
                dve.wait_ge(halves, t * 6 + 3)
                v.tensor_scalar(mean[:, one], mean[:, one], 0.5, None, ALU.mult).then_inc(halves, 1)
                v.scalar_tensor_tensor(out=spread[:, one], in0=spread[:, one], scalar=0.25, in1=spread[:, one],
                                       op0=ALU.mult, op1=ALU.mult).then_inc(halves, 1)
                v.tensor_scalar(squares[:, one], squares[:, one], 1.0 / D, EPS, ALU.mult, ALU.add).then_inc(halves, 1)

            def variance(t, p):
                one = slice(p, p + 1)
                dve.wait_ge(halves, t * 6 + 6)
                v.tensor_tensor(std[:, one], squares[:, one], spread[:, one], ALU.add).then_inc(var_ready, 1)

            def invert_std(t, p):
                dve.wait_ge(std_ready, t + 1)
                v.reciprocal(rstd[:, p:p + 1], std[:, p:p + 1]).then_inc(inverted, 1)

            def normalise(t, p):
                dve.wait_ge(inverted, t + 1)
                dve.wait_ge(stored[p], (t - p) * 8 + 16)
                v.tensor_scalar(x_out[:, p], y[:, p], mean[:, p:p + 1], rstd[:, p:p + 1], ALU.subtract,
                                ALU.mult).then_inc(normal, 1)

            def step(t, p, left, before=True):
                ahead, behind = (t + 1, 1 - p), (t - 1, 1 - p)
                if elu:
                    if left:
                        add_empty(*ahead)
                    if before:
                        count(*behind)
                    if left:
                        invert(*ahead)
                        scale(*ahead)
                    lift(t, p)
                    if left:
                        add_mean(*ahead)
                    residual(t, p)
                    if left == 0:
                        count(t, p)
                    return
                if before:
                    invert_std(*behind)
                if left:
                    add_empty(*ahead)
                if before:
                    normalise(*behind)
                residual(t, p)
                if left:
                    invert(*ahead)
                count(t, p)
                if left:
                    scale(*ahead)
                sums_of_halves(t, p)
                moments(t, p)
                variance(t, p)
                if left:
                    add_mean(*ahead)
                if left == 0:
                    invert_std(t, p)
                    normalise(t, p)

            for first in (add_empty, invert, scale, add_mean):
                first(0, 0)
            step(0, 0, 2, before=False)
            with dve.Fori(0, T // 2 - 1) as pair:
                for q in (1, 0):
                    step(pair * 2 + 2 - q, q, 2)
            step(T - 1, 1, 0)


_INS = ["x", "adj", "L0_gnn_W_self", "L0_gnn_b_self", "L0_gnn_W_nb", "L0_gnn_b_nb", "L0_gnn_W_comb", "L0_gnn_b_comb",
        "L1_gnn_W1", "L1_gnn_b1", "L1_gnn_a1", "L1_gnn_a2", "L1_gnn_b2", "L2_gnn_W", "L2_gnn_a1", "L2_gnn_a2",
        "L3_gnn_W", "L3_gnn_a"]


def kernel(**inputs):
    import numpy as _np
    import concourse.bacc as _bacc
    from concourse import mybir as _mybir
    from concourse.bass_utils import run_bass_kernel_spmd as _run

    nc = _bacc.Bacc("TRN2", target_bir_lowering=False, num_devices=1)
    arrays, args = {}, []
    for name in _INS:
        a = _np.ascontiguousarray(inputs[name]).reshape(_np.shape(inputs[name]) or (1,))
        arrays[f"in_{name}"] = a
        args.append(nc.dram_tensor(f"in_{name}", a.shape, _mybir.dt.from_np(a.dtype), kind="ExternalInput").ap())
    out = nc.dram_tensor("out", (N, D), F32, kind="ExternalOutput").ap()
    gnn_kernel(nc, *args, out)
    r = _run(nc, [arrays], core_ids=[0])
    return r.results[0]["out"]
```
